# Optimizing a Trainium2 kernel written in Bass

```python
import numpy as np
import jax
import jax.numpy as jnp

def _softmax(x, axis=-1):
    return jax.nn.softmax(x, axis=axis)

def _gelu(x):
    return jax.nn.gelu(x, approximate=True)

def _silu(x):
    return jax.nn.silu(x)

def _sigmoid(x):
    return jax.nn.sigmoid(x)

def _layernorm(x, axis=-1, eps=1e-05):
    m = jnp.mean(x, axis=axis, keepdims=True)
    v = jnp.var(x, axis=axis, keepdims=True)
    return (x - m) / jnp.sqrt(v + eps)

def _scatter_add(tgt, idx, src, axis=0):
    return tgt.at[idx].add(src)

def _segment_sum(src, seg, n):
    return jax.ops.segment_sum(src, seg, n)
kernel_name = 'mk_flamingo_gated_d1_seqx_r8_3665f5'

def setup_inputs(seed: int=0):
    np.random.seed(seed)
    _w = jnp.asarray

    def _rec_inputs():
        import jax
        import jax.numpy as jnp
        _rk = jax.random.key(seed)
        x = -0.000125 + 0.9999 * jax.random.normal(jax.random.fold_in(_rk, 1), (4, 256, 256), jnp.float32)
        _lenS = 256 - jax.random.randint(jax.random.fold_in(_rk, 7), (4,), 0, max(1, 256 // 4) + 1, jnp.int32)
        _lenS2 = 256 - jax.random.randint(jax.random.fold_in(_rk, 8), (4,), 0, max(1, 256 // 4) + 1, jnp.int32)
        itok_BxS_13_99985 = jax.random.randint(jax.random.fold_in(_rk, 11), (4, 256), 13, 99986, jnp.int32)
        _ctx_2048P = jax.random.normal(jax.random.fold_in(_rk, 12), (4, 16, 256), jnp.float32)
        _ctx_2048c = jax.random.dirichlet(jax.random.fold_in(_rk, 512), 0.3 * jnp.ones((16,), jnp.float32), (4, 256))
        _ctx_2048t = jnp.einsum('bsk,bkd->bsd', _ctx_2048c, _ctx_2048P)
        _ctx_2048t = _ctx_2048t * jax.lax.rsqrt(jnp.mean(jnp.square(_ctx_2048t)) + 1e-12) * 0.953939
        ctx_2048 = 6.82029e-06 + 0.0200006 * (_ctx_2048t + 0.3 * jax.random.normal(jax.random.fold_in(_rk, 612), (4, 256, 256), jnp.float32))
        _g = jax.random.normal(jax.random.fold_in(_rk, 9001), (2, 1), jnp.float32)
        _g = jnp.sign(_g) * jnp.maximum(jnp.abs(_g), 1.0) + (_g == 0) * 1.0
        g_xattn = _g[0]
        g_ffn = _g[1]
        return (x, itok_BxS_13_99985, ctx_2048, g_xattn, g_ffn)
    x, itok_BxS_13_99985, ctx_2048, g_xattn, g_ffn = _rec_inputs()

    def _L0_xattn_setup():
        import jax, jax.numpy as jnp
        import numpy as np
        B, S, D = (4, 512, 256)
        E = 4
        F = 1024 // E
        VOCAB = 12500
        key = jax.random.key(seed)
        k1, k2, k3, k4, k5 = jax.random.split(key, 5)
        hidden_states = jax.random.normal(k1, (B, S, D), dtype=jnp.float32)
        token_ids = jax.random.randint(k2, (B, S), 0, VOCAB, dtype=jnp.int64)
        Wg = jax.random.normal(k3, (E, F, D), dtype=jnp.float32) * 0.02
        Wu = jax.random.normal(k4, (E, F, D), dtype=jnp.float32) * 0.02
        Wd = jax.random.normal(k5, (E, D, F), dtype=jnp.float32) * 0.02
        return {'hidden_states': hidden_states, 'token_ids': token_ids, 'Wg': Wg, 'Wu': Wu, 'Wd': Wd}
    _L0_xattn_all = _L0_xattn_setup()
    _L0_xattn_in = {k: v for k, v in _L0_xattn_all.items() if k in ()}
    del _L0_xattn_all

    def _L0_ffn_setup():
        import jax, jax.numpy as jnp
        import numpy as np
        B, S, H = (4, 256, 256)
        E, I, IS = (16, 176, 704)
        TOP_K = 4
        NORM_TOPK_PROB = False

        def _routing_weights(x, router_w):
            logits = x @ router_w.T
            probs = jax.nn.softmax(logits.astype(jnp.float32), axis=-1)
            vals, idx = jax.lax.top_k(probs, TOP_K)
            if NORM_TOPK_PROB:
                vals = vals / jnp.sum(vals, axis=-1, keepdims=True)
            T = x.shape[0]
            w_dense = jnp.zeros((T, probs.shape[-1]), probs.dtype)
            w_dense = w_dense.at[jnp.arange(T)[:, None], idx].set(vals)
            return w_dense.astype(x.dtype)

        def _moe_experts(x, gate_w, up_w, down_w, w_dense):

            def body(acc, ew):
                gw, uw, dw, w = ew
                h = jax.nn.silu(x @ gw.T) * (x @ uw.T)
                return (acc + w[:, None] * (h @ dw.T), None)
            acc, _ = jax.lax.scan(body, jnp.zeros_like(x), (gate_w, up_w, down_w, w_dense.T))
            return acc
        key = jax.random.key(seed)
        ks = jax.random.split(key, 9)
        s = 0.02
        return {'hidden_states': jax.random.normal(ks[0], (B, S, H), jnp.float32), 'router_w': jax.random.normal(ks[1], (E, H), jnp.float32) * s, 'gate_w': jax.random.normal(ks[2], (E, I, H), jnp.float32) * s, 'up_w': jax.random.normal(ks[3], (E, I, H), jnp.float32) * s, 'down_w': jax.random.normal(ks[4], (E, H, I), jnp.float32) * s, 'shared_gate_w': jax.random.normal(ks[5], (IS, H), jnp.float32) * s, 'shared_up_w': jax.random.normal(ks[6], (IS, H), jnp.float32) * s, 'shared_down_w': jax.random.normal(ks[7], (H, IS), jnp.float32) * s, 'se_gate_w': jax.random.normal(ks[8], (1, H), jnp.float32) * s}
    _L0_ffn_all = _L0_ffn_setup()
    _L0_ffn_in = {k: v for k, v in _L0_ffn_all.items() if k in ('router_w', 'gate_w', 'up_w', 'down_w', 'shared_gate_w', 'shared_up_w', 'shared_down_w', 'se_gate_w')}
    del _L0_ffn_all
    return {'x': x, 'itok_BxS_13_99985': itok_BxS_13_99985, 'ctx_2048': ctx_2048, 'g_xattn': g_xattn, 'g_ffn': g_ffn, 'L0_ffn_router_w': _L0_ffn_in['router_w'], 'L0_ffn_gate_w': _L0_ffn_in['gate_w'], 'L0_ffn_up_w': _L0_ffn_in['up_w'], 'L0_ffn_down_w': _L0_ffn_in['down_w'], 'L0_ffn_shared_gate_w': _L0_ffn_in['shared_gate_w'], 'L0_ffn_shared_up_w': _L0_ffn_in['shared_up_w'], 'L0_ffn_shared_down_w': _L0_ffn_in['shared_down_w'], 'L0_ffn_se_gate_w': _L0_ffn_in['se_gate_w']}

def reference(x, itok_BxS_13_99985, ctx_2048, g_xattn, g_ffn, L0_ffn_router_w, L0_ffn_gate_w, L0_ffn_up_w, L0_ffn_down_w, L0_ffn_shared_gate_w, L0_ffn_shared_up_w, L0_ffn_shared_down_w, L0_ffn_se_gate_w):
    import jax
    import jax.numpy as jnp

    def _L0_xattn_ref(hidden_states, token_ids, Wg, Wu, Wd):
        import jax, jax.numpy as jnp
        import numpy as np
        B, S, D = (4, 512, 256)
        E = 4
        F = 1024 // E
        VOCAB = 12500
        tokens_per_expert = VOCAB // E
        tid = jnp.clip(token_ids, 0, VOCAB - 1)
        expert_ids = jnp.minimum(tid // tokens_per_expert, E - 1)
        out = jnp.zeros_like(hidden_states)
        for e in range(E):
            g = jax.nn.silu(jnp.einsum('bsd,fd->bsf', hidden_states, Wg[e]))
            u = jnp.einsum('bsd,fd->bsf', hidden_states, Wu[e])
            y = jnp.einsum('bsf,df->bsd', g * u, Wd[e])
            out = jnp.where((expert_ids == e)[..., None], y, out)
        return out

    def _L0_ffn_ref(hidden_states, router_w, gate_w, up_w, down_w, shared_gate_w, shared_up_w, shared_down_w, se_gate_w):
        import jax, jax.numpy as jnp
        import numpy as np
        B, S, H = (4, 256, 256)
        E, I, IS = (16, 176, 704)
        TOP_K = 4
        NORM_TOPK_PROB = False

        def _routing_weights(x, router_w):
            logits = x @ router_w.T
            probs = jax.nn.softmax(logits.astype(jnp.float32), axis=-1)
            vals, idx = jax.lax.top_k(probs, TOP_K)
            if NORM_TOPK_PROB:
                vals = vals / jnp.sum(vals, axis=-1, keepdims=True)
            T = x.shape[0]
            w_dense = jnp.zeros((T, probs.shape[-1]), probs.dtype)
            w_dense = w_dense.at[jnp.arange(T)[:, None], idx].set(vals)
            return w_dense.astype(x.dtype)

        def _moe_experts(x, gate_w, up_w, down_w, w_dense):

            def body(acc, ew):
                gw, uw, dw, w = ew
                h = jax.nn.silu(x @ gw.T) * (x @ uw.T)
                return (acc + w[:, None] * (h @ dw.T), None)
            acc, _ = jax.lax.scan(body, jnp.zeros_like(x), (gate_w, up_w, down_w, w_dense.T))
            return acc
        b, s, h = hidden_states.shape
        x = hidden_states.reshape(-1, h)
        w_dense = _routing_weights(x, router_w)
        moe_out = _moe_experts(x, gate_w, up_w, down_w, w_dense)
        shared = jax.nn.silu(x @ shared_gate_w.T) * (x @ shared_up_w.T) @ shared_down_w.T
        shared = jax.nn.sigmoid(x @ se_gate_w.T) * shared
        return (moe_out + shared).reshape(b, s, h)
    x = x + jnp.tanh(g_xattn[0]) * _L0_xattn_ref(_layernorm(x, axis=-1), itok_BxS_13_99985, ctx_2048, ctx_2048, ctx_2048)
    x = x + jnp.tanh(g_ffn[0]) * _L0_ffn_ref(_layernorm(x, axis=-1), L0_ffn_router_w, L0_ffn_gate_w, L0_ffn_up_w, L0_ffn_down_w, L0_ffn_shared_gate_w, L0_ffn_shared_up_w, L0_ffn_shared_down_w, L0_ffn_se_gate_w)
    return x

_drawn_inputs = setup_inputs


def setup_inputs(seed=0):
    import zlib

    import numpy as np

    out = dict(_drawn_inputs(seed))
    spreads = {}
    factors = {'L0_ffn_router_w': 8.0,
     'L0_ffn_gate_w': 8.0,
     'L0_ffn_up_w': 8.0,
     'L0_ffn_down_w': 8.0,
     'L0_ffn_shared_gate_w': 4.228,
     'L0_ffn_shared_up_w': 4.207,
     'L0_ffn_shared_down_w': 4.196,
     'L0_ffn_se_gate_w': 8.0}
    for name, (base, spread) in spreads.items():
        noise = np.random.default_rng([zlib.crc32(name.encode()), seed]).standard_normal(out[name].shape)
        drawn = base * np.exp(spread * noise) if base else spread * noise
        out[name] = jnp.asarray(drawn.astype(out[name].dtype))
    for name, factor in factors.items():
        out[name] = (out[name] * factor).astype(out[name].dtype)
    return out
```

```python
from contextlib import ExitStack

import concourse.bass as bass
from concourse import mybir

P = 128
TILES = 8
D = 256
KD = D // P
E1 = 4
E2 = 16
I2 = 176
VE = 20
TOPK = 4
IB = I2 - P
VOCAB = 12500
EPS = 1e-5

ALU = mybir.AluOpType
ACT = mybir.ActivationFunctionType
AX = mybir.AxisListType
F32 = mybir.dt.float32
I32 = mybir.dt.int32


def gated_moe_kernel(nc, x, tok, ctx_t, gates, router_t, gu_t, down_t, ident_in, out):
    with ExitStack() as ctx:
        def sb(name, shape, dt=F32):
            return ctx.enter_context(nc.sbuf_tensor(name, shape, dt))

        def sem(name):
            return ctx.enter_context(nc.semaphore(name))

        ident = sb("ident", [P, P])
        xs = sb("xs", [P, TILES, D])
        xn = sb("xn", [P, TILES, D])
        toks = sb("toks", [P, TILES], I32)
        gsb = sb("gsb", [P, 2])
        tg = sb("tg", [P, 2])
        ctxw = sb("ctxw", [P, E1, KD, D])
        rw = sb("rw", [P, KD, E2 + 1])
        gu = sb("gu", [P, VE, KD, 2 * I2])
        da = sb("da", [P, VE, D])
        db = sb("db", [IB, VE, D])
        stats = sb("stats", [P, TILES, 6])
        mv = sb("mv", [P, TILES, 2])
        std = sb("std", [P, TILES])
        rstd = sb("rstd", [P, TILES])
        ge = sb("ge", [P, E1 + 1, TILES])
        w1 = sb("w1", [P, E1, TILES])
        xT = sb("xT", [P, TILES, KD, P])
        act = sb("act", [P, 2, D])
        hid = sb("hid", [P, 2, D])
        hT = sb("hT", [P, 2, KD, P])
        lg = sb("lg", [P, TILES, E2])
        mx = sb("mx", [P, TILES])
        pr = sb("pr", [P, TILES, E2])
        rem = sb("rem", [P, TILES, E2])
        eq = sb("eq", [P, TILES, E2])
        w2 = sb("w2", [P, TILES, E2])
        rank = sb("rank", [P, E2])
        se = sb("se", [P, TILES])
        wv = sb("wv", [P, TILES, VE])

        psT = ctx.enter_context(nc.psum_tensor("psT", [P, 512], F32))
        psR = ctx.enter_context(nc.psum_tensor("psR", [P, 512], F32))
        psG = [ctx.enter_context(nc.psum_tensor(f"psG{i}", [P, 512], F32)) for i in range(2)]
        psH = [ctx.enter_context(nc.psum_tensor(f"psH{i}", [P, 512], F32)) for i in range(2)]
        psY = ctx.enter_context(nc.psum_tensor("psY", [P, 512], F32))

        s_small = sem("small_loaded")
        s_x = sem("x_loaded")
        s_ctx = sem("ctx_loaded")
        s_wts = sem("expert_weights_loaded")
        s_out = sem("out_written")
        s_v = sem("vector_step")
        s_var = sem("variance_ready")
        s_std = sem("std_ready")
        s_xn = sem("normed_ready")
        s_xt = sem("x_transposed")
        s_xtc = sem("xT_copied")
        s_mm1 = sem("inner_product_done")
        s_act = sem("silu_done")
        s_h = sem("hidden_ready")
        s_ht = sem("hidden_transposed")
        s_htc = sem("hT_copied")
        s_y = sem("y_done")
        s_res = sem("residual_done")
        s_lg = sem("logits_done")
        s_sub = sem("shifted_logits_ready")
        s_exp = sem("exp_done")
        s_tanh = sem("tanh_done")

        block = ctx.enter_context(nc.Block())

        @block.sync
        def _(sp):
            sp.dma_start(xs[:, :, :], x.rearrange("(t p) d -> p t d", p=P)).then_inc(s_x, 16)
            sp.dma_start(toks[:, :], tok).then_inc(s_small, 16)
            sp.dma_start(gsb[:, :], gates).then_inc(s_small, 16)
            sp.dma_start(ident[:, :], ident_in).then_inc(s_small, 16)
            sp.dma_start(rw[:, :, :], router_t.rearrange("(k p) n -> p k n", p=P)).then_inc(s_small, 16)
            sp.dma_start(ctxw[:, :, :, :], ctx_t.rearrange("e (k p) n -> p e k n", p=P)).then_inc(s_ctx, 16)
            for k in range(KD):
                sp.dma_start(gu[:, :, k, :], gu_t[:, k * P:(k + 1) * P, :].rearrange("e p n -> p e n")).then_inc(s_wts, 16)
            sp.dma_start(da[:, :, :], down_t[:, 0:P, :].rearrange("e p n -> p e n")).then_inc(s_wts, 16)
            sp.dma_start(db[:, :, :], down_t[:, P:I2, :].rearrange("e p n -> p e n")).then_inc(s_wts, 16)
            sp.wait_ge(s_res, 2 * TILES)
            sp.dma_start(out.rearrange("(t p) d -> p t d", p=P), xs[:, :, :]).then_inc(s_out, 16)
            sp.wait_ge(s_out, 16)

        PHASES = [(E1, D), (VE, I2)]

        @block.scalar
        def _(a):
            a.wait_ge(s_small, 64)
            a.activation(tg[:, :], gsb[:, :], ACT.Tanh).then_inc(s_tanh, 1)
            for ph, (ne, inner) in enumerate(PHASES):
                a.wait_ge(s_var, ph + 1)
                a.activation(std[:, :], mv[:, :, 1], ACT.Sqrt).then_inc(s_std, 1)
                for t in range(TILES):
                    a.wait_ge(s_xt, ph * TILES + t + 1)
                    a.activation(xT[:, t, :, :].rearrange("p k n -> p (k n)"), psT[:, 0:KD * P], ACT.Copy).then_inc(s_xtc, 1)
                if ph == 1:
                    a.wait_ge(s_sub, 1)
                    a.activation(pr[:, :, :], lg[:, :, :], ACT.Exp)
                    a.activation(se[:, :], psR[:, TILES * E2:TILES * (E2 + 1)], ACT.Exp, scale=-1.0).then_inc(s_exp, 1)
                with a.Fori(0, TILES) as t:
                    for e in range(ne):
                        n = t * ne + (ph * TILES * E1 + e)
                        a.wait_ge(s_mm1, n + 1)
                        if ph or e > 1:
                            a.wait_ge(s_h, n - 1)
                        a.activation(act[:, e % 2, 0:inner], psG[e % 2][:, 0:inner], ACT.Silu).then_inc(s_act, 1)
                        a.wait_ge(s_ht, n + 1)
                        if ph == 0:
                            a.activation(hT[:, e % 2, :, :].rearrange("p k n -> p (k n)"), psH[e % 2][:, 0:2 * P], ACT.Copy).then_inc(s_htc, 1)
                        else:
                            a.activation(hT[:, e % 2, 0, :], psH[e % 2][:, 0:P], ACT.Copy)
                            a.activation(hT[0:IB, e % 2, 1, :], psH[e % 2][0:IB, P:2 * P], ACT.Copy).then_inc(s_htc, 1)

        @block.tensor
        def _(pe):
            pe.wait_ge(s_small, 64)
            for ph, (ne, inner) in enumerate(PHASES):
                for t in range(TILES):
                    pe.wait_ge(s_xn, ph * TILES + t + 1)
                    if ph or t:
                        pe.wait_ge(s_xtc, ph * TILES + t)
                    pe.transpose(psT[:, 0:P], xn[:, t, 0:P], ident[:, :])
                    pe.transpose(psT[:, P:2 * P], xn[:, t, P:2 * P], ident[:, :]).then_inc(s_xt, 1)
                pe.wait_ge(s_xtc, (ph + 1) * TILES)
                if ph == 0:
                    pe.wait_ge(s_ctx, 16)
                else:
                    for t in range(TILES):
                        for k in range(KD):
                            pe.matmul(psR[:, t * E2:(t + 1) * E2], xT[:, t, k, :], rw[:, k, 0:E2], start=(k == 0), stop=(k == KD - 1))
                    for t in range(TILES):
                        for k in range(KD):
                            mm = pe.matmul(psR[:, TILES * E2 + t:TILES * E2 + t + 1], xT[:, t, k, :], rw[:, k, E2:E2 + 1], start=(k == 0), stop=(k == KD - 1))
                    mm.then_inc(s_lg, 1)
                    pe.wait_ge(s_wts, 64)
                for t in range(TILES):
                    base = ph * TILES * E1 + t * ne
                    for e in range(ne):
                        n = base + e
                        if n >= 2:
                            pe.wait_ge(s_h, n - 1)
                        for k in range(KD):
                            rhs = ctxw[:, e, k, :] if ph == 0 else gu[:, e, k, :]
                            mm = pe.matmul(psG[e % 2][:, 0:rhs.shape[-1]], xT[:, t, k, :], rhs, start=(k == 0), stop=(k == KD - 1))
                        mm.then_inc(s_mm1, 1)
                        pe.wait_ge(s_h, n + 1)
                        if n >= 2:
                            pe.wait_ge(s_htc, n - 1)
                        pe.transpose(psH[e % 2][:, 0:P], hid[:, e % 2, 0:P], ident[:, :])
                        pe.transpose(psH[e % 2][0:inner - P, P:2 * P], hid[:, e % 2, P:inner], ident[:, :]).then_inc(s_ht, 1)
                        pe.wait_ge(s_htc, n + 1)
                        if e == 0 and ph + t:
                            pe.wait_ge(s_res, ph * TILES + t)
                        for k in range(KD):
                            rows = P if k == 0 else inner - P
                            rhs = ctxw[:, e, k, :] if ph == 0 else (da if k == 0 else db)[:, e, :]
                            mm = pe.matmul(psY[:, 0:D], hT[0:rows, e % 2, k, :], rhs, start=(e == 0 and k == 0), stop=(e == ne - 1 and k == KD - 1))
                    mm.then_inc(s_y, 1)

        @block.vector
        def _(v):
            done = [0]

            def step(ins):
                done[0] += 1
                ins.then_inc(s_v, 1)
                v.wait_ge(s_v, done[0])

            def bc(col, n):
                return col[:, :].rearrange("p (t o) -> p t o", o=1).to_broadcast([P, TILES, n])

            v.wait_ge(s_x, 16)
            v.wait_ge(s_small, 64)
            step(v.memset(ge[:, 0, :], 1.0))
            step(v.memset(ge[:, E1, :], 0.0))
            for e in range(1, E1):
                step(v.tensor_scalar(ge[:, e, :], toks[:, :], float(e * (VOCAB // E1)), None, ALU.is_ge))
            v.wait_ge(s_tanh, 1)
            for e in range(E1):
                step(v.tensor_tensor(w1[:, e, :], ge[:, e, :], ge[:, e + 1, :], ALU.subtract))
                step(v.tensor_scalar(w1[:, e, :], w1[:, e, :], tg[:, 0:1], None, ALU.mult))
            for ph, (ne, inner) in enumerate(PHASES):
                for t in range(TILES):
                    step(v.bn_stats(stats[:, t, :], xs[:, t, :]))
                    step(v.bn_aggr(mv[:, t, :], stats[:, t, :]))
                v.tensor_scalar(mv[:, :, 1], mv[:, :, 1], EPS, None, ALU.add).then_inc(s_var, 1)
                v.wait_ge(s_std, ph + 1)
                step(v.reciprocal(rstd[:, :], std[:, :]))
                for t in range(TILES):
                    v.tensor_scalar(xn[:, t, :], xs[:, t, :], mv[:, t, 0:1], rstd[:, t:t + 1], ALU.subtract, ALU.mult).then_inc(s_xn, 1)
                if ph == 1:
                    v.wait_ge(s_lg, 1)
                    logits = psR[:, 0:TILES * E2].rearrange("p (t e) -> p t e", e=E2)
                    step(v.tensor_reduce(mx[:, :], logits, AX.X, ALU.max))
                    v.tensor_tensor(lg[:, :, :], logits, bc(mx, E2), ALU.subtract).then_inc(s_sub, 1)
                    for e in range(E2):
                        v.memset(rank[:, e:e + 1], float(E2 - e)).then_inc(s_v, 1)
                    done[0] += E2
                    v.wait_ge(s_exp, 1)
                    step(v.tensor_reduce(mx[:, :], pr[:, :, :], AX.X, ALU.add))
                    step(v.reciprocal(mx[:, :], mx[:, :]))
                    step(v.tensor_tensor(pr[:, :, :], pr[:, :, :], bc(mx, E2), ALU.mult))
                    step(v.tensor_scalar(rem[:, :, :], pr[:, :, :], 1.0, None, ALU.mult))
                    step(v.memset(w2[:, :, :], 0.0))
                    rk = rank[:, :].rearrange("p (o e) -> p o e", o=1).to_broadcast([P, TILES, E2])
                    for k in range(TOPK):
                        step(v.tensor_reduce(mx[:, :], rem[:, :, :], AX.X, ALU.max))
                        step(v.tensor_tensor(eq[:, :, :], rem[:, :, :], bc(mx, E2), ALU.is_equal))
                        step(v.tensor_tensor(eq[:, :, :], eq[:, :, :], rk, ALU.mult))
                        step(v.tensor_reduce(mx[:, :], eq[:, :, :], AX.X, ALU.max))
                        step(v.tensor_tensor(eq[:, :, :], eq[:, :, :], bc(mx, E2), ALU.is_equal))
                        step(v.tensor_tensor(w2[:, :, :], w2[:, :, :], eq[:, :, :], ALU.add))
                        step(v.scalar_tensor_tensor(rem[:, :, :], eq[:, :, :], -2.0, rem[:, :, :], ALU.mult, ALU.add))
                    step(v.tensor_tensor(w2[:, :, :], w2[:, :, :], pr[:, :, :], ALU.mult))
                    step(v.tensor_scalar(wv[:, :, 0:E2], w2[:, :, :], tg[:, 1:2], None, ALU.mult))
                    step(v.tensor_scalar(se[:, :], se[:, :], 1.0, None, ALU.add))
                    step(v.reciprocal(se[:, :], se[:, :]))
                    step(v.tensor_scalar(wv[:, :, E2:VE], bc(se, VE - E2), tg[:, 1:2], None, ALU.mult))
                for t in range(TILES):
                    for e in range(ne):
                        n = ph * TILES * E1 + t * ne + e
                        v.wait_ge(s_act, n + 1)
                        if n >= 2:
                            v.wait_ge(s_ht, n - 1)
                        w = w1[:, e, t:t + 1] if ph == 0 else wv[:, t, e:e + 1]
                        up = psG[e % 2][:, 0:D] if ph == 0 else psG[e % 2][:, I2:2 * I2]
                        v.scalar_tensor_tensor(hid[:, e % 2, 0:inner], act[:, e % 2, 0:inner], w, up, ALU.mult, ALU.mult).then_inc(s_h, 1)
                    v.wait_ge(s_y, ph * TILES + t + 1)
                    v.tensor_tensor(xs[:, t, :], psY[:, 0:D], xs[:, t, :], ALU.add).then_inc(s_res, 1)
                v.wait_ge(s_res, (ph + 1) * TILES)


def kernel(x, itok_BxS_13_99985, ctx_2048, g_xattn, g_ffn, L0_ffn_router_w, L0_ffn_gate_w, L0_ffn_up_w,
           L0_ffn_down_w, L0_ffn_shared_gate_w, L0_ffn_shared_up_w, L0_ffn_shared_down_w, L0_ffn_se_gate_w):
    import numpy as np
    import concourse.bacc as bacc
    from concourse.bass_utils import run_bass_kernel_spmd

    def chunks(w):
        return w.reshape(VE - E2, I2, D)

    gate = np.concatenate([L0_ffn_gate_w, chunks(L0_ffn_shared_gate_w)])
    up = np.concatenate([L0_ffn_up_w, chunks(L0_ffn_shared_up_w)])
    shared_down = L0_ffn_shared_down_w.reshape(D, VE - E2, I2).transpose(1, 2, 0)
    arrays = {
        "x": x.reshape(TILES * P, D),
        "tok": itok_BxS_13_99985.reshape(TILES, P).T,
        "ctx_t": ctx_2048.transpose(0, 2, 1),
        "gates": np.broadcast_to(np.concatenate([g_xattn, g_ffn]), (P, 2)),
        "router_t": np.concatenate([L0_ffn_router_w, L0_ffn_se_gate_w]).T,
        "gu_t": np.concatenate([gate, up], axis=1).transpose(0, 2, 1),
        "down_t": np.concatenate([L0_ffn_down_w.transpose(0, 2, 1), shared_down]),
        "ident_in": np.eye(P, dtype=np.float32),
    }
    nc = bacc.Bacc("TRN2", target_bir_lowering=False, num_devices=1)
    feed, args = {}, []
    for name, a in arrays.items():
        a = np.ascontiguousarray(a)
        feed[name] = a
        args.append(nc.dram_tensor(name, a.shape, mybir.dt.from_np(a.dtype), kind="ExternalInput").ap())
    args.append(nc.dram_tensor("out", (TILES * P, D), F32, kind="ExternalOutput").ap())
    gated_moe_kernel(nc, *args)
    r = run_bass_kernel_spmd(nc, [feed], core_ids=[0])
    return r.results[0]["out"].reshape(4, 256, D)
```

```python
from contextlib import ExitStack

import concourse.bass as bass
from concourse import mybir

P = 128
D = 256
KD = D // P
NT = 8
TOK = NT * P
E1, E2, TOPK = 4, 16, 4
I2 = 176
IB = I2 - P
LO = 64
CH = 4
CA = CH - 1
T1 = TOK // P + E1 - 1
T2 = (TOPK * TOK + E2 * (P - 1)) // P
J1, J2 = 12, 48
NS = CH * NT
N2 = T1 + NS
GB = T1 + NT
YB = T1 + 2 * NT
ROW = D + 2 * TOPK
VOCAB = 12500
EPS = 1e-5
NZ = E2 + 2

GU, DA, DB1, DB2 = 0, 4 * 2 * I2, 4 * 2 * I2 + 2 * D, 4 * 2 * I2 + 3 * D
SLOT = 4 * 2 * I2 + 4 * D
RAW = 2 * 2 * I2 + 2 * D
SHARED_SLOT = [12, 13, 14, 16]

ALU = mybir.AluOpType
ACT = mybir.ActivationFunctionType
AX = mybir.AxisListType
F32 = mybir.dt.float32
F32R = mybir.dt.float32r
I32 = mybir.dt.int32

C_TRI, C_ONE, C_IOTA, C_VAL, C_ROW = 0, P, 2 * P, 3 * P, 3 * P + NT
C_KEY = C_ROW + TOPK * NT
C_BEFORE = C_KEY + E2
C_END = C_BEFORE + E2 * E2
R_RANK, R_TOT, R_INV = 160, 288, 320


def f32(ap):
    return ap.bitcast(F32)


def moe_kernel(nc, x, tok, gates, ctx_w, units, router, const_a, const_b, out):
    xn1_d = nc.dram_tensor("xn1_d", (TOK, D), F32).ap()
    y1_d = nc.dram_tensor("y1_d", ((T1 + NT) * P, D), F32).ap()
    xs_d = nc.dram_tensor("xs_d", (T2 * P, ROW), F32).ap()
    y2_d = nc.dram_tensor("y2_d", ((T2 + TOPK * NT) * P, D), F32).ap()

    with ExitStack() as ctx:
        used = [0]
        total = nc.sbuf_bytes_remaining // 64 * 64 - 64
        first = -(-nc.sbuf_base // 32) * 32
        ctx.enter_context(nc.sbuf_tensor("arena", [P, total // 4], F32))

        def at(name, shape, offset, dt=F32):
            return nc.alloc_sbuf_tensor_at(name, shape, dt, offset=first + offset)

        def sb(name, shape, dt=F32):
            size = 4
            for s in shape[1:]:
                size *= s
            here, used[0] = used[0], used[0] + -(-size // 32) * 32
            assert used[0] <= total, (name, used[0], total)
            return at(name, shape, here, dt)

        W = sb("W", [P, 17, SLOT], F32R)
        stage = sb("stage", [P, 2, RAW])
        xT = sb("xT", [P, NT, 2, KD * P], F32R)
        xs = sb("xs", [P, NT, D])
        xg = sb("xg", [P, 4, ROW])
        act = sb("act", [P, 2, D])
        hid = sb("hid", [P, 2, D])
        hT = sb("hT", [P, 2, 4, P], F32R)
        ysb = sb("ysb", [P, 4, D])
        zero = sb("zero", [P, ROW])
        ca = sb("ca", [P, P + J2])
        rraw = sb("rraw", [P, KD, NZ])
        rw = sb("rw", [P, 2, KD * NZ], F32R)
        tsb = sb("tsb", [P, NT], I32)
        gsb = sb("gsb", [P, 2])
        tg = sb("tg", [P, 2])
        stats = sb("stats", [P, NT, 6])
        mv = sb("mv", [P, NT, 2])
        half = sb("half", [P, NT])
        rstd = sb("rstd", [P, NT])
        wk = sb("wk", [P, TOPK, NT])
        wse = sb("wse", [P, NT])
        gidx = sb("gidx", [P, J1], I32)
        sidx = sb("sidx", [P, J1], I32)
        posi = sb("posi", [P, TOPK * NT], I32)
        didx = sb("didx", [P, J2], I32)
        ids = sb("ids", [P, 4])
        junk = sb("junk", [P, TOPK])
        etile = sb("etile", [P, J2], I32)
        ident = ca[:, 0:P]

        cw = at("cw", [P, E1, 2, KD * D], 8 * SLOT * 4, F32R)
        off = [10 * SLOT * 4]

        def tmp(name, shape, dt=F32):
            size = 4
            for s in shape[1:]:
                size *= s
            here, off[0] = off[0], off[0] + -(-size // 32) * 32
            assert off[0] <= 12 * SLOT * 4
            return at(name, shape, here, dt)

        cb = tmp("cb", [P, C_END])
        cr = tmp("cr", [P, 2, P], F32R)
        oh = tmp("oh", [P, TOPK, NT * E2])
        lg = tmp("lg", [P, NT * E2])
        pr = tmp("pr", [P, NT * E2])
        rem = tmp("rem", [P, NT * E2])
        eq = tmp("eq", [P, NT * E2])
        sel = tmp("sel", [P, NT * E2], F32R)
        key = tmp("key", [P, NT * E2])
        cum = tmp("cum", [P, E2 * E2])
        mx = tmp("mx", [P, NT])
        ge = tmp("ge", [P, E1 + 1, NT])
        cnt = tmp("cnt", [P, 3, E2])
        cnti = tmp("cnti", [P, 2, E2], I32)
        posf = tmp("posf", [P, 3, TOPK * NT])
        posj = tmp("posj", [P, 2, TOPK * NT], I32)
        bm = tmp("bm", [P, NT, P], F32R)
        am = tmp("am", [P, NT, J1], F32R)
        le = tmp("le", [P, J2, E2])
        lesum = tmp("lesum", [P, J2])
        xn = at("xn", [P, NT, ROW], 15 * SLOT * 4)
        fin = at("fin", [P, 4, TOPK, D], 0)

        def bank(name):
            return ctx.enter_context(nc.psum_tensor(name, [P, 512], F32))

        psX, psR = bank("psX"), bank("psR")
        psG = [bank(f"psG{i}") for i in range(2)]
        psH = [bank(f"psH{i}") for i in range(2)]
        psY = [bank(f"psY{i}") for i in range(2)]

        def sem(name):
            return ctx.enter_context(nc.semaphore(name))

        s_tok, s_cb, s_gate, s_ca, s_rw = (sem(n) for n in ("tok_in", "const_b_in", "gates_in", "const_a_in", "router_in"))
        s_x = [sem(f"x_in{i}") for i in range(2)]
        s_stage = [sem(f"stage_in{i}") for i in range(2)]
        s_xn1d = sem("xn1_stored")
        s_gath = [sem(f"gathered{i}") for i in range(4)]
        s_scat = [sem(f"y1_scattered{i}") for i in range(4)]
        s_y1 = [sem(f"y1_loaded{i}") for i in range(NT)]
        s_zero = sem("zero_tile")
        s_zfill = sem("sorted_rows_zeroed")
        s_rows = sem("rows_sorted")
        s_ld = [sem(f"sorted_rows_in{i}") for i in range(4)]
        s_scat2 = [sem(f"y2_scattered{i}") for i in range(4)]
        s_fin = [sem(f"results_in{i}") for i in range(4)]
        s_out = sem("out_stored")
        s_cr = sem("routing_consts_rounded")
        s_rwhi, s_rwlo = sem("router_hi"), sem("router_lo")
        s_whi, s_wlo = sem("unit_hi"), sem("unit_lo")
        s_tanh = sem("tanh_done")
        s_v = sem("vector_chain")
        s_half = sem("exponent_set")
        s_var = sem("variance_ready")
        s_rstd = sem("rstd_ready")
        s_xn = sem("normed")
        s_sel = sem("selection_ready")
        s_rank = sem("ranks_done")
        s_ab = sem("one_hots_ready")
        s_inv = sem("inverse_done")
        s_idx = sem("tile_indices_ready")
        s_xt, s_xhi, s_xlo = sem("x_transposed"), sem("xT_hi"), sem("xT_lo")
        s_mm1, s_act, s_hid = sem("inner_done"), sem("silu_done"), sem("hidden_ready")
        s_ht, s_hthi, s_htlo = sem("hidden_transposed"), sem("hT_hi"), sem("hT_lo")
        s_mm2 = sem("outer_done")
        s_y1sb = sem("y1_copied")
        s_yacc = sem("shared_added")
        s_y2sb = sem("y2_copied")
        s_lgt, s_sub, s_exp = sem("logits_done"), sem("logits_shifted"), sem("exp_done")
        s_pos = sem("positions_ready")
        s_et = sem("tile_experts_ready")
        s_id, s_didx = sem("ids_ready"), sem("dest_ready")
        s_comb = sem("combined")

        block = ctx.enter_context(nc.Block())

        NU = 2 + CH + E2

        def shared_step(s):
            return (s % CA, s // CA) if s < CA * NT else (CA, s - CA * NT)

        def group(n):
            if n < T1:
                return n
            c, t = shared_step(n - T1)
            return T1 + t if c < CA else T1 + NT + t

        SPLIT_0 = [0, 1]
        SPLIT_1 = {1: [2], 3: [3], 5: [4], 7: [5], 9: [6]}
        SPLIT_B = [7, 8, 9]
        SPLIT_S = {0: [], 2: [10], 5: [11], 11: [12], 15: [13], 18: [14], 21: [15],
                   23: [16], 24: [17], 26: [18], 27: [19], 29: [20], 31: [21]}
        LN_AT = {s: s + 2 for s in range(6)}

        def unit_slot(u):
            return SHARED_SLOT[u - 2] if u < 2 + CH else u - 2 - CH

        def free_slot(eng, u):
            slot = unit_slot(u)
            if u < 2 + CH:
                return
            if slot in (8, 9):
                eng.wait_ge(s_mm2, T1)
            if slot in (10, 11):
                eng.wait_ge(s_et, 1)
            if slot in (12, 13, 14):
                eng.wait_ge(s_mm2, T1 + CA * NT)
            if slot == 15:
                eng.wait_ge(s_rows, 16 * TOPK * NT)

        @block.sync
        def _(sp):
            def load_unit(u):
                if u >= 2:
                    sp.wait_ge(s_wlo, u - 1)
                if u < 2:
                    sp.dma_start(stage[:, u, 0:2 * KD * D], ctx_w[u]).then_inc(s_stage[u % 2], 16)
                else:
                    sp.dma_start(stage[:, u % 2, :], units[u - 2]).then_inc(s_stage[u % 2], 16)

            sp.dma_start(tsb[:, :], tok).then_inc(s_tok, 16)
            sp.dma_start(cb[:, :], const_b).then_inc(s_cb, 16)
            xv = x.rearrange("(t p) d -> p t d", p=P)
            for h in range(2):
                sp.dma_start(xs[:, 4 * h:4 * h + 4, :], xv[:, 4 * h:4 * h + 4, :]).then_inc(s_x[h], 16)
            sp.dma_start(ca[:, :], const_a).then_inc(s_ca, 16)
            sp.dma_start(gsb[:, :], gates).then_inc(s_gate, 16)
            load_unit(0)
            load_unit(1)
            sp.dma_start(rraw[:, :, :], router).then_inc(s_rw, 16)
            sp.wait_ge(s_xn, NT)
            sp.dma_start(xn1_d.rearrange("(t p) d -> p t d", p=P), xn[:, :, 0:D]).then_inc(s_xn1d, 16)
            for u in range(2, 7):
                load_unit(u)
            sp.wait_ge(s_zero, 1)
            sp.dma_start(xs_d.rearrange("(j p) d -> p j d", p=P),
                         zero[:, :].rearrange("p (o d) -> p o d", o=1).to_broadcast([P, T2, ROW])).then_inc(s_zfill, 16)
            for u in range(7, 9):
                load_unit(u)
            for i in range(4):
                sp.wait_ge(s_scat[i], 16 * len(range(i, T1, 4)))
            for t in range(NT):
                sp.dma_start(xn[:, t, 0:D], y1_d[(T1 + t) * P:(T1 + t + 1) * P, :]).then_inc(s_y1[t], 16)
            for u in range(9, NU):
                load_unit(u)
            for i in range(4):
                if i == 0:
                    sp.wait_ge(s_rows, 16 * TOPK * NT)
                sp.dma_start(xg[:, i, :], xs_d[i * P:(i + 1) * P, :]).then_inc(s_ld[i], 16)
            def load_rows(j, i):
                sp.wait_ge(s_id, j - 3)
                sp.dma_start(xg[:, i, :], xs_d[bass.ds(j * P, P), :]).then_inc(s_ld[i], 16)

            with sp.Fori(1, T2 // 4) as r:
                for i in range(4):
                    load_rows(r * 4 + i, i)
            for j in range(T2 // 4 * 4, T2):
                load_rows(j, j % 4)
            sp.wait_ge(s_mm2, N2 + T2)
            for i in range(4):
                sp.wait_ge(s_scat2[i], 16 * len(range(i, T2, 4)))
            yv = y2_d[T2 * P:(T2 + TOPK * NT) * P, :].rearrange("(k t p) d -> t p k d", k=TOPK, p=P)
            ov = out.rearrange("(t p) d -> p t d", p=P)
            for t in range(NT):
                if t >= 4:
                    sp.wait_ge(s_comb, t - 3)
                sp.dma_start(fin[:, t % 4, :, :], yv[t]).then_inc(s_fin[t % 4], 16)
            for t in range(0, NT, 2):
                sp.wait_ge(s_comb, t + 2)
                sp.dma_start(ov[:, t:t + 2, :], xs[:, t:t + 2, :]).then_inc(s_out, 16)
            sp.wait_ge(s_out, 16 * NT // 2)

        @block.gpsimd
        def _(pool):
            pool.memset(zero[:, :], 0.0).then_inc(s_zero, 1)
            pool.memset(half[:, :], -0.5).then_inc(s_half, 1)
            pool.wait_ge(s_half, 1)
            for h in range(2):
                pool.wait_ge(s_var, h + 1)
                pool.tensor_tensor(rstd[:, 4 * h:4 * h + 4], mv[:, 4 * h:4 * h + 4, 1], half[:, 0:4], ALU.pow).then_inc(s_rstd, 1)

            def scatter1(j):
                pool.wait_ge(s_y1sb, j + 1)
                pool.indirect_dma_start(y1_d, bass.IndirectOffsetOnAxis(ap=sidx[:, j:j + 1], axis=0), ysb[:, j % 4, :], None).then_inc(s_scat[j % 4], 16)

            pool.wait_ge(s_idx, 1)
            pool.wait_ge(s_xn1d, 16)
            for j in range(T1):
                if j >= 4:
                    pool.wait_ge(s_xt, j - 3)
                pool.indirect_dma_start(xg[:, j % 4, 0:D], None, xn1_d, bass.IndirectOffsetOnAxis(ap=gidx[:, j:j + 1], axis=0)).then_inc(s_gath[j % 4], 16)
                if j >= 5:
                    scatter1(j - 5)
            for j in range(T1 - 5, T1):
                scatter1(j)
            for t in range(NT):
                pool.wait_ge(s_var, 2 + t + 1)
                pool.tensor_tensor(rstd[:, t:t + 1], mv[:, t, 1:2], half[:, 0:1], ALU.pow).then_inc(s_rstd, 1)
            pool.wait_ge(s_pos, 2)
            pool.wait_ge(s_zfill, 16)
            for c in range(TOPK * NT):
                pool.indirect_dma_start(xs_d, bass.IndirectOffsetOnAxis(ap=posi[:, c:c + 1], axis=0), xn[:, c % NT, :], None).then_inc(s_rows, 16)
            for j in range(T2):
                pool.wait_ge(s_y2sb, j + 1)
                pool.wait_ge(s_didx, j + 1)
                pool.indirect_dma_start(y2_d, bass.IndirectOffsetOnAxis(ap=didx[:, j:j + 1], axis=0), ysb[:, j % 4, :], None).then_inc(s_scat2[j % 4], 16)

        @block.scalar
        def _(a):
            def split_hi(u):
                a.wait_ge(s_stage[u % 2], 16 * (u // 2 + 1))
                st = stage[:, u % 2, :]
                if u < 2:
                    a.activation(cw[:, 2 * u:2 * u + 2, 0, :], st[:, 0:2 * KD * D].rearrange("p (e n) -> p e n", e=2), ACT.Copy).then_inc(s_whi, 1)
                    return
                slot = unit_slot(u)
                free_slot(a, u)
                a.activation(W[:, slot, GU:GU + KD * 2 * I2], st[:, 0:KD * 2 * I2], ACT.Copy)
                a.activation(W[:, slot, DA:DA + D], st[:, KD * 2 * I2:KD * 2 * I2 + D], ACT.Copy)
                a.activation(W[0:LO + IB, slot, DB1:DB1 + D], st[0:LO + IB, KD * 2 * I2 + D:RAW], ACT.Copy).then_inc(s_whi, 1)

            def x_hi(g, slot, free=None):
                a.wait_ge(s_xt, g + 1)
                if free is not None:
                    a.wait_ge(s_mm1, free)
                a.activation(xT[:, slot, 0, :], psX[:, 0:KD * P], ACT.Copy).then_inc(s_xhi, 1)

            def silu(n, u, width, later=True):
                a.wait_ge(s_mm1, n + 1)
                if later:
                    a.wait_ge(s_hid, n - 1)
                a.activation(act[:, u, 0:width], psG[u][:, 0:width], ACT.Silu).then_inc(s_act, 1)

            def hT_hi(n, u, packed, later=True):
                a.wait_ge(s_ht, n + 1)
                if later:
                    a.wait_ge(s_mm2, n - 1)
                a.activation(hT[:, u, 0, :], psH[u][:, 0:P], ACT.Copy)
                r = IB if packed else P
                a.activation(hT[0:r, u, 2, :], psH[u][0:r, P:2 * P], ACT.Copy).then_inc(s_hthi, 1)

            def y1_out(j):
                a.wait_ge(s_mm2, j + 1)
                if j >= 4:
                    a.wait_ge(s_scat[j % 4], 16 * (j // 4))
                a.activation(ysb[:, j % 4, :], psY[j % 2][:, 0:D], ACT.Copy).then_inc(s_y1sb, 1)

            def y2_out(j, i, group4):
                a.wait_ge(s_mm2, j + (N2 + 1))
                if not (isinstance(group4, int) and group4 == 0):
                    a.wait_ge(s_scat2[i], group4 * 16)
                a.activation(ysb[:, i, :], psY[(YB + i) % 2][:, 0:D], ACT.Copy).then_inc(s_y2sb, 1)

            a.wait_ge(s_cb, 16)
            a.activation(cr[:, :, :].rearrange("p a n -> p (a n)"), cb[:, 0:2 * P], ACT.Copy).then_inc(s_cr, 1)
            a.wait_ge(s_gate, 16)
            a.activation(tg[:, :], gsb[:, :], ACT.Tanh).then_inc(s_tanh, 1)
            for u in SPLIT_0:
                split_hi(u)
            a.wait_ge(s_rw, 16)
            a.activation(rw[:, 0, :], rraw[:, :, :].rearrange("p k n -> p (k n)"), ACT.Copy).then_inc(s_rwhi, 1)
            x_hi(0, 0)
            x_hi(1, 1)
            for n in range(T1):
                silu(n, n % 2, D, n >= 2)
                if n >= 1:
                    hT_hi(n - 1, (n - 1) % 2, False, n >= 3)
                if n + 2 < T1:
                    x_hi(n + 2, (n + 2) % NT, n + 2 - NT + 1 if n + 2 >= NT else None)
                if n >= 2:
                    y1_out(n - 2)
                for u in SPLIT_1.get(n, []):
                    split_hi(u)
            hT_hi(T1 - 1, (T1 - 1) % 2, False)
            y1_out(T1 - 2)
            y1_out(T1 - 1)
            for u in SPLIT_B:
                split_hi(u)
            x_hi(T1, 0, T1)
            x_hi(T1 + 1, 1)
            for s in range(NS):
                n = T1 + s
                silu(n, n % 2, I2)
                if s >= 1:
                    hT_hi(n - 1, (n - 1) % 2, True)
                if s in LN_AT:
                    x_hi(T1 + LN_AT[s], LN_AT[s])
                if s == 7:
                    a.wait_ge(s_sub, 1)
                    a.activation(pr[:, :], lg[:, :], ACT.Exp)
                    a.activation(wse[:, :], psR[:, 0:NT * NZ].rearrange("p (t z) -> p t z", z=NZ)[:, :, E2], ACT.Exp, scale=-1.0).then_inc(s_exp, 1)
                for u in SPLIT_S.get(s, []):
                    split_hi(u)
                if s >= NS - 2:
                    j = s - (NS - 2)
                    x_hi(GB + j, j, T1 + CA * NT + j + 1)

            def tile(i, k, q):
                known = isinstance(i, int)
                if not known or i < T2:
                    silu(i + N2, (N2 + k) % 2, I2)
                if not known or i - 1 < T2:
                    hT_hi(i + (N2 - 1), (N2 + k - 1) % 2, True)
                if not known or i + 2 < T2:
                    x_hi(i + (GB + 2), k % 2, i + (N2 + 1))
                if not known or i >= 2:
                    y2_out(i - 2, (k - 2) % 4, q)

            for i in range(6):
                tile(i, i % 4, (i - 2) // 4)
            with a.Fori(1, 10) as r:
                for k in range(4):
                    tile(r * 4 + (2 + k), (2 + k) % 4, r)
            for i in range(42, T2 + 2):
                tile(i, i % 4, (i - 2) // 4)

        @block.tensor
        def _(pe):
            def x_transpose(g, src):
                if not (isinstance(g, int) and g == 0):
                    pe.wait_ge(s_xlo, g)
                pe.transpose(psX[:, 0:P], src[:, 0:P], ident)
                pe.transpose(psX[:, P:2 * P], src[:, P:2 * P], ident).then_inc(s_xt, 1)

            def inner(n, g, slot, u, hi, lo, later=True):
                pe.wait_ge(s_xlo, g + 1)
                if later:
                    pe.wait_ge(s_hid, n - 1)
                width = hi(0).shape[-1]
                for k in range(KD):
                    b = slice(k * P, (k + 1) * P)
                    pe.matmul(psG[u][:, 0:width], xT[:, slot, 0, b], hi(k), start=(k == 0), stop=False)
                    pe.matmul(psG[u][:, 0:width], xT[:, slot, 0, b], lo(k), start=False, stop=False)
                    mm = pe.matmul(psG[u][:, 0:width], xT[:, slot, 1, b], hi(k), start=False, stop=(k == KD - 1))
                mm.then_inc(s_mm1, 1)

            def transpose(n, u, width, later=True):
                pe.wait_ge(s_hid, n + 1)
                if later:
                    pe.wait_ge(s_htlo, n - 1)
                pe.transpose(psH[u][:, 0:P], hid[:, u, 0:P], ident)
                pe.transpose(psH[u][0:width - P, P:2 * P], hid[:, u, P:width], ident).then_inc(s_ht, 1)

            def outer1(n):
                u, e = n % 2, slice(0, D)
                pe.wait_ge(s_htlo, n + 1)
                if n >= 2:
                    pe.wait_ge(s_y1sb, n - 1)
                for k in range(KD):
                    pe.matmul(psY[u][:, 0:D], hT[:, u, 2 * k, :], cwv(n, 0, k), start=(k == 0), stop=False)
                    pe.matmul(psY[u][:, 0:D], hT[:, u, 2 * k, :], cwv(n, 1, k), start=False, stop=False)
                    mm = pe.matmul(psY[u][:, 0:D], hT[:, u, 2 * k + 1, :], cwv(n, 0, k), start=False, stop=(k == KD - 1))
                mm.then_inc(s_mm2, 1)

            def outer2(n, u, y, w, start=True, stop=True):
                pe.wait_ge(s_htlo, n + 1)
                R = LO + IB
                o = psY[y][:, 0:D]
                pe.matmul(o, hT[:, u, 0, :], w(P, DA, D), start=start, stop=False)
                pe.matmul(o, hT[:, u, 0, :], w(P, DA + D, D), start=False, stop=False)
                pe.matmul(o, hT[:, u, 1, :], w(P, DA, D), start=False, stop=False)
                pe.matmul(o, hT[0:R, u, 2, :], w(R, DB1, D), start=False, stop=False)
                pe.matmul(o, hT[0:IB, u, 2, :], w(IB, DB2, D), start=False, stop=stop).then_inc(s_mm2, 1)

            tile_e = {}

            def cwv(n, part, k):
                e = tile_e[n]
                return cw[:, bass.ds(e, 1), part, k * D:(k + 1) * D].rearrange("p o n -> p (o n)")

            def static_w(slot):
                return lambda rows, a, n: W[0:rows, slot, a:a + n]

            def expert_w(e):
                return lambda rows, a, n: W[0:rows, bass.ds(e, 1), a:a + n].rearrange("p o n -> p (o n)")

            def halves(w):
                return (lambda k: w(P, GU + k * 2 * I2, 2 * I2)), (lambda k: w(P, GU + (KD + k) * 2 * I2, 2 * I2))

            def ranks(e, times):
                pe.wait_ge(s_sel, times)
                tri, one = cr[:, 0, :], cr[:, 1, :]
                w = NT * e
                pe.matmul(psR[:, R_RANK:R_RANK + w], tri, sel[:, 0:w], start=True, stop=False, skip_group_check=True)
                for t in range(NT - 1):
                    m = NT - 1 - t
                    pe.matmul(psR[:, R_RANK + (t + 1) * e:R_RANK + w].rearrange("p (m e) -> p m e", e=e), one,
                              sel[:, t * e:(t + 1) * e].rearrange("p (o e) -> p o e", o=1).to_broadcast([P, m, e]),
                              start=False, stop=(t == NT - 2), skip_group_check=True)
                for t in range(NT):
                    mm = pe.matmul(psR[:, R_TOT:R_TOT + e], one, sel[:, t * e:(t + 1) * e], start=(t == 0), stop=(t == NT - 1))
                mm.then_inc(s_rank, 1)

            pe.wait_ge(s_cr, 1)
            ranks(E1, 1)
            pe.wait_ge(s_ab, 1)
            for c in range(NT):
                mm = pe.matmul(psR[:, R_INV:R_INV + J1], bm[:, c, :], am[:, c, :], start=(c == 0), stop=(c == NT - 1))
            mm.then_inc(s_inv, 1)
            pe.wait_ge(s_ca, 16)
            pe.wait_ge(s_idx, 1)

            def gathered(j):
                pe.wait_ge(s_gath[j % 4], 16 * (j // 4 + 1))
                return xg[:, j % 4, :]

            x_transpose(0, gathered(0))
            x_transpose(1, gathered(1))
            pe.wait_ge(s_wlo, len(SPLIT_0))
            for n in range(T1):
                tile_e[n] = pe.value_load(etile[0:1, n:n + 1], min_val=0, max_val=E1 - 1)
                inner(n, n, n % NT, n % 2, lambda k: cwv(n, 0, k), lambda k: cwv(n, 1, k), n >= 2)
                if n >= 1:
                    transpose(n - 1, (n - 1) % 2, D, n >= 3)
                if n + 2 < T1:
                    x_transpose(n + 2, gathered(n + 2))
                if n >= 2:
                    outer1(n - 2)
            transpose(T1 - 1, (T1 - 1) % 2, D)
            outer1(T1 - 2)
            outer1(T1 - 1)

            def token_tile(t):
                pe.wait_ge(s_xn, NT + t + 1)
                return xn[:, t, :]

            def logits(t):
                if t == 0:
                    pe.wait_ge(s_rwlo, 1)
                pe.wait_ge(s_xlo, T1 + t + 1)
                for k in range(KD):
                    b, z = slice(k * P, (k + 1) * P), slice(k * NZ, (k + 1) * NZ)
                    o = psR[:, t * NZ:(t + 1) * NZ]
                    pe.matmul(o, xT[:, t, 0, b], rw[:, 0, z], start=(k == 0), stop=False)
                    pe.matmul(o, xT[:, t, 0, b], rw[:, 1, z], start=False, stop=False)
                    mm = pe.matmul(o, xT[:, t, 1, b], rw[:, 0, z], start=False, stop=(k == KD - 1))
                mm.then_inc(s_lgt, 1)

            def outer_shared(n):
                c, t = shared_step(n - T1)
                g = group(n)
                if c == 0 or c == CA:
                    if g < T1 + 2:
                        pe.wait_ge(s_y1sb, T1)
                    else:
                        pe.wait_ge(s_yacc, g - T1 - 1)
                outer2(n, n % 2, g % 2, static_w(SHARED_SLOT[c]), start=(c in (0, CA)), stop=(c >= CA - 1))

            def loaded(i, q):
                pe.wait_ge(s_ld[i], q * 16 + 16)
                return xg[:, i, :]

            x_transpose(T1, token_tile(0))
            x_transpose(T1 + 1, token_tile(1))
            for s in range(NS):
                n = T1 + s
                c, t = shared_step(s)
                if t == 0:
                    pe.wait_ge(s_wlo, 2 + c + 1)
                inner(n, T1 + t, t, n % 2, *halves(static_w(SHARED_SLOT[c])))
                if s >= 1:
                    transpose(n - 1, (n - 1) % 2, I2)
                if s < NT:
                    logits(s)
                if s in LN_AT:
                    x_transpose(T1 + LN_AT[s], token_tile(LN_AT[s]))
                if s == 13:
                    ranks(E2, 2)
                if s >= NS - 2:
                    x_transpose(GB + s - (NS - 2), loaded(s - (NS - 2), 0))
                if s >= 2:
                    outer_shared(n - 2)

            def expert(j):
                col = etile[0:1, j:j + 1] if isinstance(j, int) else etile[0:1, bass.ds(j, 1)]
                return pe.value_load(col, min_val=0, max_val=E2 - 1)

            def tile(i, k, q):
                known = isinstance(i, int)
                if not known or i < T2:
                    e = expert(i)
                    pe.wait_ge(s_wlo, e + (2 + CH + 1))
                    inner(i + N2, i + GB, k % 2, (N2 + k) % 2, *halves(expert_w(e)))
                if not known or i - 1 < T2:
                    transpose(i + (N2 - 1), (N2 + k - 1) % 2, I2)
                if not known or i + 2 < T2:
                    x_transpose(i + (GB + 2), loaded((k + 2) % 4, q))
                if known and i < 2:
                    outer_shared(N2 + i - 2)
                    return
                e = expert(i - 2)
                if known and i < 4:
                    pe.wait_ge(s_yacc, 2 * NT - 1 + i - 2)
                else:
                    pe.wait_ge(s_y2sb, i - 3)
                outer2(i + (N2 - 2), (N2 + k) % 2, (YB + k) % 2, expert_w(e))

            pe.wait_ge(s_et, 1)
            for i in range(6):
                tile(i, i % 4, (i + 2) // 4)
            with pe.Fori(1, 10) as r:
                for k in range(4):
                    tile(r * 4 + (2 + k), (2 + k) % 4, r + 1)
            for i in range(42, T2 + 2):
                tile(i, i % 4, (i + 2) // 4)

        @block.vector
        def _(v):
            done = [0]

            def step(ins, more=()):
                for i in (ins, *more):
                    i.then_inc(s_v, 1)
                    done[0] += 1
                v.wait_ge(s_v, done[0])

            def mid(ap, n, m):
                return ap.rearrange("p (o m) -> p o m", o=1).to_broadcast([P, n, m])

            def last(ap, n, m):
                return ap.rearrange("p (n o) -> p n o", o=1).to_broadcast([P, n, m])

            def positions(e, k, times):
                v.wait_ge(s_rank, times)
                step(v.tensor_scalar(cnti[:, 0, 0:e], psR[:, R_TOT:R_TOT + e], float(P - 1), None, ALU.add))
                step(v.tensor_scalar(cnti[:, 1, 0:e], cnti[:, 0, 0:e], 7, None, ALU.arith_shift_right))
                step(v.tensor_copy(cnt[:, 0, 0:e], cnti[:, 1, 0:e]))
                c3 = cum[:, 0:e * e].rearrange("p (a b) -> p a b", b=e)
                before = cb[:, C_BEFORE:C_END].rearrange("p (a b) -> p a b", b=E2)[:, 0:e, 0:e]
                step(v.tensor_tensor(c3, before, mid(cnt[:, 0, 0:e], e, e), ALU.mult))
                step(v.tensor_reduce(cnt[:, 1, 0:e], c3, AX.X, ALU.add))
                w = NT * e
                step(v.scalar_tensor_tensor(key[:, 0:w].rearrange("p (t e) -> p t e", e=e), mid(cnt[:, 1, 0:e], NT, e), float(P),
                                            psR[:, R_RANK:R_RANK + w].rearrange("p (t e) -> p t e", e=e), ALU.mult, ALU.add))
                for i in range(k):
                    step(v.tensor_tensor(eq[:, 0:w], oh[:, i, 0:w], key[:, 0:w], ALU.mult))
                    step(v.tensor_reduce(posf[:, 0, i * NT:(i + 1) * NT], eq[:, 0:w].rearrange("p (t e) -> p t e", e=e), AX.X, ALU.add))
                step(v.tensor_copy(posi[:, 0:k * NT], posf[:, 0, 0:k * NT]))

            def tile_experts(e, j):
                l3 = le[0:1, 0:j, 0:e]
                start = cnt[0:1, 1, 0:e].rearrange("p (o m) -> p o m", o=1).to_broadcast([1, j, e])
                col = cb[0:1, C_IOTA:C_IOTA + j].rearrange("p (n o) -> p n o", o=1).to_broadcast([1, j, e])
                step(v.tensor_tensor(l3, start, col, ALU.is_le))
                step(v.tensor_reduce(lesum[0:1, 0:j], l3, AX.X, ALU.add))
                return v.tensor_scalar(etile[0:1, 0:j], lesum[0:1, 0:j], -1.0, None, ALU.add)

            def moments(t0, n):
                step(v.bn_stats(stats[:, t0, :], xs[:, t0, :]), [v.bn_stats(stats[:, t, :], xs[:, t, :]) for t in range(t0 + 1, t0 + n)])
                step(v.bn_aggr(mv[:, t0, :], stats[:, t0, :]), [v.bn_aggr(mv[:, t, :], stats[:, t, :]) for t in range(t0 + 1, t0 + n)])
                v.tensor_scalar(mv[:, t0:t0 + n, 1], mv[:, t0:t0 + n, 1], EPS, None, ALU.add).then_inc(s_var, 1)

            def normalise(t):
                v.tensor_scalar(xn[:, t, 0:D], xs[:, t, :], mv[:, t, 0:1], rstd[:, t:t + 1], ALU.subtract, ALU.mult).then_inc(s_xn, 1)

            def split_lo(u):
                v.wait_ge(s_whi, u + 1)
                st = stage[:, u % 2, :]
                if u < 2:
                    v.tensor_tensor(cw[:, 2 * u:2 * u + 2, 1, :], st[:, 0:2 * KD * D].rearrange("p (e n) -> p e n", e=2),
                                    f32(cw[:, 2 * u:2 * u + 2, 0, :]), ALU.subtract).then_inc(s_wlo, 1)
                    return
                slot, g = unit_slot(u), KD * 2 * I2
                v.tensor_tensor(W[:, slot, GU + g:GU + 2 * g], st[:, 0:g], f32(W[:, slot, GU:GU + g]), ALU.subtract)
                v.tensor_tensor(W[:, slot, DA + D:DA + 2 * D], st[:, g:g + D], f32(W[:, slot, DA:DA + D]), ALU.subtract)
                v.tensor_tensor(W[0:IB, slot, DB2:DB2 + D], st[0:IB, g + D:RAW], f32(W[0:IB, slot, DB1:DB1 + D]), ALU.subtract).then_inc(s_wlo, 1)

            def x_lo(g, slot):
                v.wait_ge(s_xhi, g + 1)
                v.tensor_tensor(xT[:, slot, 1, :], psX[:, 0:KD * P], f32(xT[:, slot, 0, :]), ALU.subtract).then_inc(s_xlo, 1)

            def hidden(n, u, up, width, later=True):
                v.wait_ge(s_act, n + 1)
                if later:
                    v.wait_ge(s_ht, n - 1)
                v.tensor_tensor(hid[:, u, 0:width], act[:, u, 0:width], psG[u][:, up:up + width], ALU.mult).then_inc(s_hid, 1)

            def hT_lo(n, u, packed):
                v.wait_ge(s_hthi, n + 1)
                v.tensor_tensor(hT[:, u, 1, :], psH[u][:, 0:P], f32(hT[:, u, 0, :]), ALU.subtract)
                if packed:
                    v.tensor_tensor(hT[LO:LO + IB, u, 2, :], psH[u][0:IB, P:2 * P], f32(hT[0:IB, u, 2, :]), ALU.subtract).then_inc(s_htlo, 1)
                else:
                    v.tensor_tensor(hT[:, u, 3, :], psH[u][:, P:2 * P], f32(hT[:, u, 2, :]), ALU.subtract).then_inc(s_htlo, 1)

            v.wait_ge(s_tok, 16)
            v.wait_ge(s_cb, 16)
            step(v.memset(ge[:, 0, :], 1.0), [v.memset(ge[:, E1, :], 0.0)] +
                 [v.tensor_scalar(ge[:, e, :], tsb[:, :], float(e * (VOCAB // E1)), None, ALU.is_ge) for e in range(1, E1)])
            w1 = NT * E1
            step(v.tensor_tensor(oh[:, 0, 0:w1].rearrange("p (t e) -> p e t", e=E1), ge[:, 0:E1, :], ge[:, 1:E1 + 1, :], ALU.subtract))
            v.tensor_copy(sel[:, 0:w1], oh[:, 0, 0:w1]).then_inc(s_sel, 1)
            positions(E1, 1, 1)
            step(v.tensor_scalar(posj[:, 0, 0:NT], posi[:, 0:NT], P - 1, None, ALU.bitwise_and),
                 [v.tensor_scalar(posj[:, 1, 0:NT], posi[:, 0:NT], 7, None, ALU.arith_shift_right)])
            step(v.tensor_copy(posf[:, 1, 0:NT], posj[:, 0, 0:NT]), [v.tensor_copy(posf[:, 2, 0:NT], posj[:, 1, 0:NT])])
            step(v.tensor_tensor(am[:, :, :], mid(cb[:, C_IOTA:C_IOTA + J1], NT, J1), last(posf[:, 2, 0:NT], NT, J1), ALU.is_equal),
                 [v.tensor_tensor(bm[:, :, :], mid(cb[:, C_IOTA:C_IOTA + P], NT, P), last(posf[:, 1, 0:NT], NT, P), ALU.is_equal)])
            v.tensor_tensor(am[:, :, :], f32(am[:, :, :]), last(cb[:, C_VAL:C_VAL + NT], NT, J1), ALU.mult).then_inc(s_ab, 1)
            step(tile_experts(E1, J1))
            v.wait_ge(s_ca, 16)
            v.wait_ge(s_inv, 1)
            inv = psR[:, R_INV:R_INV + J1]
            step(v.tensor_scalar(gidx[:, :], inv, float(-T1 * P), 0.0, ALU.add, ALU.max))
            v.tensor_tensor(sidx[:, :], inv, ca[:, P:P + J1], ALU.max).then_inc(s_idx, 1)
            for h in range(2):
                v.wait_ge(s_x[h], 16)
                moments(4 * h, 4)
            for t in range(NT):
                if t % 4 == 0:
                    v.wait_ge(s_rstd, t // 4 + 1)
                normalise(t)
            for u in SPLIT_0:
                split_lo(u)
            v.wait_ge(s_rwhi, 1)
            v.tensor_tensor(rw[:, 1, :], rraw[:, :, :].rearrange("p k n -> p (k n)"), f32(rw[:, 0, :]), ALU.subtract).then_inc(s_rwlo, 1)
            x_lo(0, 0)
            x_lo(1, 1)
            for n in range(T1):
                hidden(n, n % 2, 0, D, n >= 2)
                if n >= 1:
                    hT_lo(n - 1, (n - 1) % 2, False)
                if n + 2 < T1:
                    x_lo(n + 2, (n + 2) % NT)
                for u in SPLIT_1.get(n, []):
                    split_lo(u)
            hT_lo(T1 - 1, (T1 - 1) % 2, False)
            v.wait_ge(s_mm2, T1)
            v.wait_ge(s_zero, 1)
            step(v.tensor_copy(hT[32:LO, 0, 2, :], zero[32:LO, 0:P]), [v.tensor_copy(hT[32:LO, 1, 2, :], zero[32:LO, 0:P])])
            for u in SPLIT_B:
                split_lo(u)

            def residual(t):
                v.wait_ge(s_y1[t], 16)
                step(v.scalar_tensor_tensor(xs[:, t, :], xn[:, t, 0:D], tg[:, 0:1], xs[:, t, :], ALU.mult, ALU.add))
                moments(t, 1)

            def second_norm(t):
                v.wait_ge(s_rstd, 2 + t + 1)
                normalise(t)

            v.wait_ge(s_tanh, 1)
            residual(0)
            residual(1)
            second_norm(0)
            residual(2)
            second_norm(1)
            x_lo(T1, 0)
            x_lo(T1 + 1, 1)

            def add_shared(n):
                c, t = shared_step(n - T1)
                if c in (CA - 1, CA):
                    g = group(n)
                    v.wait_ge(s_mm2, n + 1)
                    v.wait_ge(s_yacc, g - T1) if g > T1 else None
                    v.scalar_tensor_tensor(xs[:, t, :], psY[g % 2][:, 0:D], wse[:, t:t + 1], xs[:, t, :], ALU.mult, ALU.add).then_inc(s_yacc, 1)

            t3 = lambda ap: ap.rearrange("p (t e) -> p t e", e=E2)

            def shifted_logits():
                v.wait_ge(s_lgt, NT)
                z = psR[:, 0:NT * NZ].rearrange("p (t z) -> p t z", z=NZ)[:, :, 0:E2]
                step(v.tensor_reduce(mx[:, :], z, AX.X, ALU.max))
                v.tensor_tensor(t3(lg[:, :]), z, last(mx[:, :], NT, E2), ALU.subtract).then_inc(s_sub, 1)
                v.wait_ge(s_exp, 1)
                step(v.tensor_scalar(wse[:, :], wse[:, :], 1.0, None, ALU.add))
                step(v.reciprocal(wse[:, :], wse[:, :]))
                step(v.tensor_scalar(wse[:, :], wse[:, :], tg[:, 1:2], None, ALU.mult))

            def probabilities():
                step(v.tensor_reduce(mx[:, :], t3(pr[:, :]), AX.X, ALU.add))
                step(v.reciprocal(mx[:, :], mx[:, :]))
                step(v.tensor_tensor(t3(rem[:, :]), t3(pr[:, :]), last(mx[:, :], NT, E2), ALU.mult))

            def choose(k):
                step(v.tensor_reduce(mx[:, :], t3(rem[:, :]), AX.X, ALU.max))
                v.tensor_scalar(wk[:, k, :], mx[:, :], tg[:, 1:2], None, ALU.mult).then_inc(s_v, 1)
                done[0] += 1
                step(v.tensor_tensor(t3(eq[:, :]), t3(rem[:, :]), last(mx[:, :], NT, E2), ALU.is_equal))
                step(v.tensor_tensor(t3(eq[:, :]), t3(eq[:, :]), mid(cb[:, C_KEY:C_KEY + E2], NT, E2), ALU.mult))
                step(v.tensor_reduce(mx[:, :], t3(eq[:, :]), AX.X, ALU.max))
                step(v.tensor_tensor(t3(oh[:, k, :]), t3(eq[:, :]), last(mx[:, :], NT, E2), ALU.is_equal))
                step(v.scalar_tensor_tensor(rem[:, :], oh[:, k, :], -2.0, rem[:, :], ALU.mult, ALU.add))

            def selection():
                step(v.tensor_tensor(eq[:, :], oh[:, 0, :], oh[:, 1, :], ALU.add))
                step(v.tensor_tensor(key[:, :], oh[:, 2, :], oh[:, 3, :], ALU.add))
                v.tensor_tensor(sel[:, :], eq[:, :], key[:, :], ALU.add).then_inc(s_sel, 1)

            def sorted_places():
                positions(E2, TOPK, 2)
                v.tensor_copy(xn[:, :, D:D + TOPK].rearrange("p t k -> p k t"),
                              posf[:, 0, :].rearrange("p (k t) -> p k t", k=TOPK)).then_inc(s_pos, 1)
                v.tensor_copy(xn[:, :, D + TOPK:ROW].rearrange("p t k -> p k t"),
                              cb[:, C_ROW:C_ROW + TOPK * NT].rearrange("p (k t) -> p k t", k=TOPK)).then_inc(s_pos, 1)

            def dest(j, i):
                col = ca[:, P + j:P + j + 1] if isinstance(j, int) else ca[:, bass.ds(j + P, 1)]
                to = didx[:, j:j + 1] if isinstance(j, int) else didx[:, bass.ds(j, 1)]
                v.scalar_tensor_tensor(junk[:, :], xg[:, i, D:D + TOPK], col, xg[:, i, D + TOPK:ROW], ALU.is_equal, ALU.mult,
                                       accum_out=ids[:, i:i + 1]).then_inc(s_id, 1)
                v.wait_ge(s_id, j + 1)
                v.tensor_scalar(to, ids[:, i:i + 1], col, None, ALU.max).then_inc(s_didx, 1)

            for s in range(NS):
                n = T1 + s
                hidden(n, n % 2, I2, I2)
                if s >= 1:
                    hT_lo(n - 1, (n - 1) % 2, True)
                if s in LN_AT:
                    second_norm(LN_AT[s])
                    x_lo(T1 + LN_AT[s], LN_AT[s])
                    if LN_AT[s] + 1 < NT:
                        residual(LN_AT[s] + 1)
                if s == 7:
                    shifted_logits()
                    for m in range(T1, n - 1):
                        add_shared(m)
                if s == 8:
                    probabilities()
                if 8 <= s < 12:
                    choose(s - 8)
                if s == 12:
                    selection()
                if s == 14:
                    sorted_places()
                if s == 15:
                    tile_experts(E2, J2).then_inc(s_et, 1)
                if s >= 8:
                    add_shared(n - 2)
                for u in SPLIT_S.get(s, []):
                    split_lo(u)
                if s >= NS - 2:
                    x_lo(GB + s - (NS - 2), s - (NS - 2))
                    dest(s - (NS - 2), s - (NS - 2))

            def tile(i, k):
                known = isinstance(i, int)
                if not known or i < T2:
                    hidden(i + N2, (N2 + k) % 2, I2, I2)
                if not known or i - 1 < T2:
                    hT_lo(i + (N2 - 1), (N2 + k - 1) % 2, True)
                if not known or i + 2 < T2:
                    x_lo(i + (GB + 2), k % 2)
                    dest(i + 2, (k + 2) % 4)
                if known and i < 2:
                    add_shared(N2 + i - 2)

            for i in range(6):
                tile(i, i % 4)
            with v.Fori(1, 10) as r:
                for k in range(4):
                    tile(r * 4 + (2 + k), (2 + k) % 4)
            for i in range(42, T2 + 1):
                tile(i, i % 4)
            for t in range(NT):
                v.wait_ge(s_fin[t % 4], 16 * (t // 4 + 1))
                for k in range(TOPK):
                    ins = v.scalar_tensor_tensor(xs[:, t, :], fin[:, t % 4, k, :], wk[:, k, t:t + 1], xs[:, t, :], ALU.mult, ALU.add)
                    if k < TOPK - 1:
                        step(ins)
                ins.then_inc(s_comb, 1)


def kernel(x, itok_BxS_13_99985, ctx_2048, g_xattn, g_ffn, L0_ffn_router_w, L0_ffn_gate_w, L0_ffn_up_w,
           L0_ffn_down_w, L0_ffn_shared_gate_w, L0_ffn_shared_up_w, L0_ffn_shared_down_w, L0_ffn_se_gate_w):
    import numpy as np
    import concourse.bacc as bacc
    from concourse.bass_utils import run_bass_kernel_spmd

    def blocks(w):
        n, _, c = w.shape
        return w.reshape(n, KD, P, c).transpose(0, 2, 1, 3).reshape(n, P, KD * c)

    def chunks(w):
        return w.reshape(CH, I2, D)

    gate = np.concatenate([chunks(L0_ffn_shared_gate_w), L0_ffn_gate_w])
    up = np.concatenate([chunks(L0_ffn_shared_up_w), L0_ffn_up_w])
    down = np.concatenate([L0_ffn_shared_down_w.reshape(D, CH, I2).transpose(1, 2, 0), L0_ffn_down_w.transpose(0, 2, 1)])
    units = np.zeros((CH + E2, P, RAW), np.float32)
    units[:, :, 0:KD * 2 * I2] = blocks(np.concatenate([gate, up], axis=1).transpose(0, 2, 1))
    units[:, :, KD * 2 * I2:KD * 2 * I2 + D] = down[:, 0:P]
    for row in (0, LO):
        units[:, row:row + IB, KD * 2 * I2 + D:] = down[:, P:]
    ctx_t = blocks(ctx_2048.transpose(0, 2, 1)).reshape(2, 2, P, KD * D).transpose(0, 2, 1, 3).reshape(2, P, 2 * KD * D)
    router = np.concatenate([L0_ffn_router_w, L0_ffn_se_gate_w, L0_ffn_se_gate_w[:1]]).T
    lane = np.arange(P, dtype=np.float32)
    const_a = np.zeros((P, P + J2), np.float32)
    const_a[:, 0:P] = np.eye(P)
    const_a[:, P:] = np.arange(J2) * P + lane[:, None]
    const_b = np.zeros((P, C_END), np.float32)
    const_b[:, C_TRI:C_TRI + P] = lane[:, None] < lane
    const_b[:, C_ONE:C_ONE + P] = 1
    const_b[:, C_IOTA:C_IOTA + P] = lane
    const_b[:, C_VAL:C_VAL + NT] = (T1 + np.arange(NT)) * P + lane[:, None]
    const_b[:, C_ROW:C_ROW + TOPK * NT] = (T2 + np.arange(TOPK * NT)) * P + lane[:, None]
    const_b[:, C_KEY:C_KEY + E2] = E2 - np.arange(E2)
    const_b[:, C_BEFORE:] = (np.arange(E2)[:, None] > np.arange(E2)).reshape(-1)
    arrays = {
        "x": x.reshape(TOK, D),
        "tok": itok_BxS_13_99985.reshape(NT, P).T,
        "gates": np.broadcast_to(np.concatenate([g_xattn, g_ffn]), (P, 2)),
        "ctx_w": ctx_t,
        "units": units,
        "router": router.reshape(KD, P, NZ).transpose(1, 0, 2),
        "const_a": const_a,
        "const_b": const_b,
    }
    nc = bacc.Bacc("TRN2", target_bir_lowering=False, num_devices=1, dynamic_dma_scratch_size=8192)
    feed, args = {}, []
    for name, a in arrays.items():
        a = np.ascontiguousarray(a)
        feed[name] = a
        args.append(nc.dram_tensor(name, a.shape, mybir.dt.from_np(a.dtype), kind="ExternalInput").ap())
    args.append(nc.dram_tensor("out", (TOK, D), F32, kind="ExternalOutput").ap())
    moe_kernel(nc, *args)
    r = run_bass_kernel_spmd(nc, [feed], core_ids=[0])
    return r.results[0]["out"].reshape(4, 256, D)
```

```python
from contextlib import ExitStack

import concourse.bass as bass
from concourse import mybir

P = 128
D = 256
KD = D // P
NT = 8
TOK = NT * P
E1, E2, TOPK = 4, 16, 4
I2 = 176
IB = I2 - P
LO = 64
CH = 4
CA = CH - 1
T1 = NT + E1 - 1
T2 = (TOPK * TOK + E2 * (P - 1)) // P
J1, J2 = T1 + 1, T2 + 1
BEFORE = NT // 2
N2 = T1 + CA * NT + BEFORE
N3 = N2 + T2
N = N3 + NT - BEFORE
GB = T1 + NT
YB = T1 + NT + BEFORE
LATE = E2 - TOPK + 1
G = 4
EARLY = G + NT
RING = 8
S1 = 6
WARM = 20
VOCAB = 12500
EPS = 1e-5
NZ = E2 + 2

DA, DB1, DB2 = 4 * 2 * I2, 4 * 2 * I2 + 2 * D, 4 * 2 * I2 + 3 * D
SLOT = 4 * 2 * I2 + 4 * D
RAW = 2 * 2 * I2 + 2 * D
SB = 2
SHARED_SLOT = [12, 13, 14, 16]

ALU = mybir.AluOpType
ACT = mybir.ActivationFunctionType
AX = mybir.AxisListType
F32 = mybir.dt.float32
F32R = mybir.dt.float32r
I32 = mybir.dt.int32

C_TRI, C_ONE, C_IOTA, C_ROW1, C_ROW2 = 0, P, 2 * P, 3 * P, 3 * P + NT
C_BEFORE = C_ROW2 + TOPK * NT
C_THR = C_BEFORE + E2 * E2
C_START = C_THR + S1
C_END = C_START + J2
R_RANK, R_TOT, R_INV = 160, 288, 432


def f32(ap):
    return ap.bitcast(F32)


def moe_kernel(nc, x, tok, gates, ctx_w, units, router, const_a, const_b, out):
    xn_d = nc.dram_tensor("xn_d", (TOK, D), F32).ap()
    y_d = nc.dram_tensor("y_d", ((TOPK * NT + T2) * P, D), F32).ap()

    with ExitStack() as ctx:
        used = [0]
        total = nc.sbuf_bytes_remaining // 64 * 64 - 64
        first = -(-nc.sbuf_base // 32) * 32
        ctx.enter_context(nc.sbuf_tensor("arena", [P, total // 4], F32))

        def at(name, shape, offset, dt=F32):
            return nc.alloc_sbuf_tensor_at(name, shape, dt, offset=first + offset)

        def sb(name, shape, dt=F32):
            size = 4
            for s in shape[1:]:
                size *= s
            here, used[0] = used[0], used[0] + -(-size // 32) * 32
            assert used[0] <= total, (name, used[0], total)
            return at(name, shape, here, dt)

        W = sb("W", [P, E2 + 1, SLOT], F32R)
        stage = sb("stage", [P, SB, RAW])
        xT = sb("xT", [P, NT, 2, KD * P], F32R)
        xs = sb("xs", [P, NT, D])
        xg = sb("xg", [P, G, D])
        act = sb("act", [P, 2, D])
        hid = sb("hid", [P, 2, D])
        hT = sb("hT", [P, 2, 5, P], F32R)
        ysb = sb("ysb", [P, 4, D])
        ca = sb("ca", [P, P + 1 + J2])
        rraw = sb("rraw", [P, KD, NZ])
        rw = sb("rw", [P, 2, KD * NZ], F32R)
        tsb = sb("tsb", [P, NT], I32)
        gsb = sb("gsb", [P, 2])
        tg = sb("tg", [P, 2])
        stats = sb("stats", [P, NT, 6])
        mv = sb("mv", [P, 2, NT, 2])
        half = sb("half", [P, 1])
        rstd = sb("rstd", [P, 2, NT])
        shift = sb("shift", [P, 2, NT])
        mask = sb("mask", [P, J1])
        wk = sb("wk", [P, TOPK, NT])
        wse = sb("wse", [P, NT])
        gidx = sb("gidx", [P, NT], I32)
        gidx2 = sb("gidx2", [P, J2], I32)
        didx = sb("didx", [P, J2], I32)
        tile1 = sb("tile1", [P, 2, J1], I32)
        etile = sb("etile", [P, J2], I32)
        ident = ca[:, 0:P]
        lane = ca[:, P:P + 1]

        cw = at("cw", [P, E1, 2, KD * D], 8 * SLOT * 4, F32R)
        off = [10 * SLOT * 4]

        def tmp(name, shape, dt=F32):
            size = 4
            for s in shape[1:]:
                size *= s
            here, off[0] = off[0], off[0] + -(-size // 32) * 32
            assert off[0] <= 12 * SLOT * 4
            return at(name, shape, here, dt)

        cb = tmp("cb", [P, C_END])
        cr = tmp("cr", [P, 2, P], F32R)
        oh = tmp("oh", [P, TOPK, NT * E2])
        best = tmp("best", [P, NT, 8])
        which = tmp("which", [P, NT, 8], mybir.dt.uint32)
        lg = tmp("lg", [P, NT, E2 + TOPK + 1])
        pr = tmp("pr", [P, NT, E2 + TOPK + 1])
        eq2 = tmp("eq2", [P, NT * E2])
        eq = tmp("eq", [P, NT * E2])
        sel = tmp("sel", [P, NT * E2], F32R)
        key = tmp("key", [P, NT * E2])
        cum = tmp("cum", [P, E2 * E2])
        mx = tmp("mx", [P, NT])
        lt = tmp("lt", [P, NT, S1], F32R)
        starts = tmp("starts", [P, S1])
        sm = tmp("sm", [P, 4, J1])
        sm3 = tmp("sm3", [P, J1, E1 - 1])
        cnt = tmp("cnt", [P, 2, E2])
        cnti = tmp("cnti", [P, 2, E2], I32)
        posi = tmp("posi", [P, TOPK * NT], I32)
        posj = tmp("posj", [P, TOPK * NT], I32)
        start = tmp("start", [P, TOPK * NT])
        started = tmp("started", [E2, J2], F32R)
        bm = tmp("bm", [P, 2, NT // 2, P], F32R)
        am = tmp("am", [P, 2, NT // 2, J2], F32R)
        inv = tmp("inv", [P, 2, J2])
        xn = at("xn", [P, NT, D], 15 * SLOT * 4)
        fin = at("fin", [P, NT, TOPK, D], 0)
        diag = at("diag", [P, 2, TOPK, P], 4 * SLOT * 4)

        def bank(name):
            return ctx.enter_context(nc.psum_tensor(name, [P, 512], F32))

        psR = bank("psR")
        psX = bank("psX")
        psG = [bank(f"psG{i}") for i in range(2)]
        psH = [bank(f"psH{i}") for i in range(2)]
        psYb = [bank(f"psY{i}") for i in range(2)]

        def psY(y):
            return psYb[y % 2][:, 0:D]

        def sem(name):
            return ctx.enter_context(nc.semaphore(name))

        s_tok, s_cb, s_gate, s_ca, s_rw = (sem(n) for n in ("tok_in", "const_b_in", "gates_in", "const_a_in", "router_in"))
        s_stage = [sem(f"stage_in{i}") for i in range(SB)]
        s_x = [sem(f"token_tile_in{i}") for i in range(NT)]
        s_cr = sem("routing_consts_rounded")
        s_rwhi, s_rwlo = sem("router_hi"), sem("router_lo")
        s_whi, s_wlo, s_wlo_pool = sem("unit_hi"), sem("unit_lo"), sem("unit_lo_by_pool")
        s_tanh = sem("tanh_done")
        s_v = sem("vector_chain")
        s_sel, s_rank = sem("selection_ready"), sem("ranks_done")
        s_ab, s_inv = sem("one_hots_ready"), sem("inverse_step_done")
        s_idx, s_pairs = sem("token_order_ready"), sem("first_moe_steps_ready")
        s_half, s_var, s_rstd = sem("exponent_set"), sem("variance_ready"), sem("rstd_ready")
        s_shift, s_shift2 = sem("shift_ready"), sem("second_shift_ready")
        s_xs = [sem(f"residual_started{i}") for i in range(NT)]
        s_xn1, s_xn = sem("first_normed"), sem("second_normed")
        s_xnd = sem("normed_stored")
        s_zero = sem("packed_gap_zeroed")
        s_started, s_count = sem("experts_started"), sem("started_experts_counted")
        s_idx2, s_et = sem("sorted_rows_known"), sem("tile_experts_ready")
        s_early = [sem(f"early_rows_in{i}") for i in range(EARLY)]
        s_gath = [sem(f"sorted_rows_in{i}") for i in range(RING)]
        s_scat = [sem(f"y_scattered{i}") for i in range(4)]
        s_fin = [sem(f"results_in{i}") for i in range(NT)]
        s_out = sem("out_stored")
        s_xt, s_xhi, s_xlo = sem("x_transposed"), sem("xT_hi"), sem("xT_lo")
        s_mm1, s_act, s_hid = sem("inner_done"), sem("silu_done"), sem("hidden_ready")
        s_ht, s_hthi, s_htlo = sem("hidden_transposed"), sem("hT_hi"), sem("hT_lo")
        s_mm2 = sem("outer_done")
        s_yacc = sem("outer_added")
        s_ysb = sem("y_copied")
        s_lgt, s_sub, s_exp = sem("logits_done"), sem("logits_shifted"), sem("exp_done")
        s_diag, s_sum = sem("diagonals_ready"), sem("results_summed")
        s_comb = sem("combined")

        block = ctx.enter_context(nc.Block())

        NU = 2 + CH + E2

        def second(n):
            return N2 <= n < N3

        def shared_step(n):
            s = n - T1 if n < N2 else n - T1 - T2
            return (s % CA, s // CA) if s < CA * NT else (CA, s - CA * NT)

        def y_group(n):
            if n < T1:
                return n
            if second(n):
                return YB + n - N2
            c, t = shared_step(n)
            return T1 + t if c < CA else T1 + NT + t + (T2 if n >= N3 else 0)

        def y_edges(n):
            if n < T1 or second(n):
                return True, True
            c, _ = shared_step(n)
            return c in (0, CA), c >= CA - 1

        def x_group(n):
            if n < T1:
                return n
            return GB + n - N2 if second(n) else T1 + shared_step(n)[1]

        def x_slot(g):
            if g < T1:
                return NT - 3 + g % 3
            return g - T1 if g < GB else (g - GB) % 2

        def x_at(n):
            if n == 0:
                return [1, 2]
            if n < GB - 2:
                return [n + 2]
            return [GB + n + 2 - N2] if second(n + 2) else []

        def last_use(g):
            before = [n for n in range(N3) if x_group(n) < g and x_slot(x_group(n)) == x_slot(g)]
            return max(before) if before else None

        def wait_y_read(eng, y):
            if YB <= y < YB + T2:
                eng.wait_ge(s_ysb, y - YB + 1)
            else:
                eng.wait_ge(s_yacc, y + 1 - (T2 if y > YB else 0))

        def rows_of(j):
            if j < EARLY:
                return xn[:, j - G, :] if j >= G else xg[:, j, :]
            i = (j - EARLY) % RING
            return xg[:, i, :] if i < G else f32(xT[:, 2 + (i - G) // 2, (i - G) % 2, :])

        def rows_sem(j):
            return (s_early[j], 16) if j < EARLY else (s_gath[(j - EARLY) % RING], 16 * ((j - EARLY) // RING + 1))

        RANKS_AT, INVERSE_AT = 10, 15

        SPLIT_AT = {-1: [0, 1, 2], 1: [3], 4: [4], 7: [5], 10: [6], T1: [7], T1 + 2: [8], T1 + 4: [9], T1 + 6: [10],
                    T1 + 8: [11], T1 + 11: [12], T1 + 14: [13], T1 + 17: [14], T1 + 20: [15], T1 + 23: [16],
                    T1 + 24: [17], T1 + 26: [18]}
        POOL_LO = [0, 2, 3, 4, 5, 6, 7, 8, 9, 10, 11, 12, 13, 14, 15]
        HI_AT = {n - 2 + m: (u, m) for n, u in ((4, 4), (7, 5)) for m in range(3)}
        LATE_AT = {N2 + 6 * i + m + (1 if i < 2 else 2): (2 + CH + LATE + i, m) for i in range(TOPK - 1) for m in range(3)}
        HI_AT.update(LATE_AT)
        LO_AT = {n + 3: part for n, part in LATE_AT.items()}

        def wait_unit(eng, u):
            if u in POOL_LO:
                eng.wait_ge(s_wlo_pool, POOL_LO.index(u) + 1)
            else:
                eng.wait_ge(s_wlo, u - sum(p < u for p in POOL_LO) + 1)

        def unit_slot(u):
            return SHARED_SLOT[u - 2] if u < 2 + CH else u - 2 - CH

        BY_PE = range(1, NT, 2)

        def mid(ap, n, m):
            return ap.rearrange("p (o m) -> p o m", o=1).to_broadcast([P, n, m])

        def last(ap, n, m):
            return ap.rearrange("p (n o) -> p n o", o=1).to_broadcast([P, n, m])

        def lo_parts(u):
            st = stage[:, u % SB, :]
            if u < 2:
                w = cw[:, 2 * u:2 * u + 2, :, :]
                return [(w[:, :, 1, :], w[:, :, 0, :], st[:, 0:2 * KD * D].rearrange("p (e n) -> p e n", e=2))]
            w, g = W[:, unit_slot(u), :], KD * 2 * I2
            return [(w[:, g:2 * g], w[:, 0:g], st[:, 0:g]),
                    (w[:, DA + D:DA + 2 * D], w[:, DA:DA + D], st[:, g:g + D]),
                    (w[0:IB, DB2:DB2 + D], w[0:IB, DB1:DB1 + D], st[0:IB, g + D:RAW])]

        def wait_slot_free(eng, u):
            slot = unit_slot(u)
            if u < 2 + CH:
                return
            if slot in (8, 9):
                eng.wait_ge(s_mm2, T1)
            if slot in SHARED_SLOT:
                eng.wait_ge(s_mm2, T1 + CA * (NT - 1) + SHARED_SLOT.index(slot) + 1)
            if slot in (10, 11):
                eng.wait_ge(s_idx2, 1)
            if slot == 15:
                eng.wait_ge(s_xt, GB + EARLY)

        @block.sync
        def _(sp):
            def load_unit(u):
                if u >= SB:
                    wait_unit(sp, u - SB)
                if u < 2:
                    sp.dma_start(stage[:, u, 0:2 * KD * D], ctx_w[u]).then_inc(s_stage[u % SB], 16)
                else:
                    sp.dma_start(stage[:, u % SB, :], units[u - 2]).then_inc(s_stage[u % SB], 16)

            sp.dma_start(tsb[:, :], tok).then_inc(s_tok, 16)
            sp.dma_start(cb[:, :], const_b).then_inc(s_cb, 16)
            sp.dma_start(ca[:, :], const_a).then_inc(s_ca, 16)
            sp.dma_start(gsb[:, :], gates).then_inc(s_gate, 16)
            sp.dma_start(rraw[:, :, :], router).then_inc(s_rw, 16)
            for u in range(NU):
                load_unit(u)
            sp.wait_ge(s_mm2, N3)
            for i in range(4):
                sp.wait_ge(s_scat[i], 16 * len(range(i, T2, 4)))
            yv = y_d[0:TOPK * TOK, :].rearrange("(k t p) d -> t p k d", k=TOPK, p=P)
            for t in range(NT):
                sp.dma_start(fin[:, t, :, :], yv[t]).then_inc(s_fin[t], 16)

        @block.gpsimd
        def _(pool):
            def rsqrt(h, t):
                pool.wait_ge(s_var, h * NT + t + 1)
                pool.tensor_tensor(rstd[:, h, t:t + 1], mv[:, h, t, 1:2], half[:, :], ALU.pow).then_inc(s_rstd, 1)

            def gather_tokens(t):
                pool.indirect_dma_start(xn[:, t, :], None, x, bass.IndirectOffsetOnAxis(ap=gidx[:, t:t + 1], axis=0)).then_inc(s_x[t], 16)

            def split_lo(u):
                pool.wait_ge(s_whi, u + 1)
                for dst, hi, src in lo_parts(u):
                    ins = pool.tensor_tensor(dst, src, f32(hi), ALU.subtract)
                ins.then_inc(s_wlo_pool, 1)

            def gather_sorted(j):
                if j >= EARLY + RING:
                    pool.wait_ge(s_xt, GB + j - RING + 1)
                elif j >= EARLY + G:
                    pool.wait_ge(s_mm1, N2)
                elif j >= EARLY:
                    pool.wait_ge(s_xt, GB + j - EARLY + 1)
                pool.indirect_dma_start(rows_of(j), None, xn_d, bass.IndirectOffsetOnAxis(ap=gidx2[:, j:j + 1], axis=0)).then_inc(rows_sem(j)[0], 16)

            def scatter(j):
                pool.wait_ge(s_ysb, j + 1)
                pool.indirect_dma_start(y_d, bass.IndirectOffsetOnAxis(ap=didx[:, j:j + 1], axis=0), ysb[:, j % 4, :], None).then_inc(s_scat[j % 4], 16)

            pool.memset(half[:, :], -0.5).then_inc(s_half, 1)
            pool.wait_ge(s_half, 1)
            split_lo(0)
            pool.wait_ge(s_idx, 1)
            for t in range(NT // 2):
                gather_tokens(t)
            rsqrt(0, 0)
            rsqrt(0, 1)
            gather_tokens(4)
            gather_tokens(5)
            rsqrt(0, 2)
            gather_tokens(6)
            gather_tokens(7)
            rsqrt(0, 3)
            split_lo(2)
            rsqrt(0, 4)
            rsqrt(0, 5)
            split_lo(3)
            rsqrt(0, 6)
            rsqrt(0, 7)
            for n in range(T1 + INVERSE_AT + 2 * TOPK):
                if 0 <= n - E1 - 1 < NT:
                    rsqrt(1, n - E1 - 1)
                for u in SPLIT_AT.get(n, []):
                    if u in POOL_LO and n > 1:
                        split_lo(u)
            pool.wait_ge(s_idx2, 1)
            pool.wait_ge(s_xnd, 16 * NT)
            pool.wait_ge(s_xt, GB)
            for j in range(EARLY):
                gather_sorted(j)
            for j in range(T2 + 4):
                if j < G:
                    gather_sorted(EARLY + j)
                    gather_sorted(EARLY + G + j)
                if EARLY + RING <= j + RING < T2:
                    gather_sorted(j + RING)
                if j >= 4:
                    scatter(j - 4)
            for t in range(NT):
                pool.wait_ge(s_comb, t + 1)
                pool.indirect_dma_start(out, bass.IndirectOffsetOnAxis(ap=gidx[:, t:t + 1], axis=0), xs[:, t, :], None).then_inc(s_out, 16)
            pool.wait_ge(s_out, 16 * NT)

        @block.scalar
        def _(a):
            def split_hi(u, parts=(0, 1, 2)):
                st, g = stage[:, u % SB, :], KD * 2 * I2
                if parts[0] == 0:
                    a.wait_ge(s_stage[u % SB], 16 * (u // SB + 1))
                    wait_slot_free(a, u)
                if u < 2:
                    a.activation(cw[:, 2 * u:2 * u + 2, 0, :], st[:, 0:2 * KD * D].rearrange("p (e n) -> p e n", e=2), ACT.Copy).then_inc(s_whi, 1)
                    return
                w = W[:, unit_slot(u), :]
                if 0 in parts:
                    a.activation(w[:, 0:g], st[:, 0:g], ACT.Copy)
                if 1 in parts:
                    a.activation(w[:, DA:DA + D], st[:, g:g + D], ACT.Copy)
                if 2 in parts:
                    a.activation(w[0:LO + IB, DB1:DB1 + D], st[0:LO + IB, g + D:RAW], ACT.Copy).then_inc(s_whi, 1)

            def x_hi(g):
                a.wait_ge(s_xt, g + 1)
                if last_use(g) is not None:
                    a.wait_ge(s_mm1, last_use(g) + 1)
                a.activation(xT[:, x_slot(g), 0, :], psX[:, 0:D], ACT.Copy).then_inc(s_xhi, 1)

            def silu(n):
                width = D if n < T1 else I2
                a.wait_ge(s_mm1, n + 1)
                if n >= 2:
                    a.wait_ge(s_hid, n - 1)
                a.activation(act[:, n % 2, 0:width], psG[n % 2][:, 0:width], ACT.Silu).then_inc(s_act, 1)

            def hT_hi(n):
                a.wait_ge(s_ht, n + 1)
                if n >= 2:
                    a.wait_ge(s_mm2, n - 1)
                u = n % 2
                if n < T1:
                    hi = hT[:, u, 0:4, :].rearrange("p (k h) n -> p k h n", h=2)[:, :, 0, :]
                    a.activation(hi, psH[u][:, 0:D].rearrange("p (k n) -> p k n", k=KD), ACT.Copy).then_inc(s_hthi, 1)
                else:
                    a.activation(hT[:, u, 0, :], psH[u][:, 0:P], ACT.Copy)
                    a.activation(hT[0:IB, u, 4, :], psH[u][0:IB, P:2 * P], ACT.Copy).then_inc(s_hthi, 1)

            def first_norm(n):
                if n == 0:
                    a.wait_ge(s_pairs, 1)
                t = a.value_load(tile1[0:1, 1, n:n + 1], min_val=0, max_val=NT - 1)
                a.wait_ge(s_shift, min(n + 1, NT))
                if n >= G:
                    a.wait_ge(s_xt, n - G + 1)
                a.activation(xg[:, n % G, :], xn[:, bass.ds(t, 1), :].rearrange("p o n -> p (o n)"), ACT.Identity,
                             bias=shift[:, 0, bass.ds(t, 1)], scale=rstd[:, 0, bass.ds(t, 1)]).then_inc(s_xn1, 1)

            def y_out(j):
                a.wait_ge(s_mm2, N2 + j + 1)
                if j >= 4:
                    a.wait_ge(s_scat[j % 4], 16 * (j // 4))
                a.activation(ysb[:, j % 4, :], psY(YB + j), ACT.Copy).then_inc(s_ysb, 1)

            a.wait_ge(s_cb, 16)
            a.activation(act[:, 0, 0:1], cb[:, 0:1], ACT.Silu)
            a.activation(cr[:, :, :].rearrange("p a n -> p (a n)"), cb[:, 0:2 * P], ACT.Copy).then_inc(s_cr, 1)
            a.wait_ge(s_gate, 16)
            a.activation(tg[:, :], gsb[:, :], ACT.Tanh).then_inc(s_tanh, 1)
            a.wait_ge(s_rw, 16)
            a.activation(rw[:, 0, :], rraw[:, :, :].rearrange("p k n -> p (k n)"), ACT.Copy).then_inc(s_rwhi, 1)
            split_hi(0)
            split_hi(1)
            split_hi(2)
            first_norm(0)
            x_hi(0)
            first_norm(1)
            first_norm(2)
            for n in range(N + 2):
                if n < N:
                    silu(n)
                if 1 <= n <= N:
                    hT_hi(n - 1)
                for g in x_at(n):
                    x_hi(g)
                if n < T1 - 3:
                    first_norm(n + 3)
                if n < NT:
                    a.wait_ge(s_x[n], 16)
                    a.dma_start(xs[:, n, :], xn[:, n, :]).then_inc(s_xs[n], 16)
                if 0 <= n - E1 - 4 < NT:
                    t = n - E1 - 4
                    a.wait_ge(s_shift2, t + 1)
                    a.activation(xn[:, t, :], xs[:, t, :], ACT.Identity, bias=shift[:, 1, t:t + 1], scale=rstd[:, 1, t:t + 1]).then_inc(s_xn, 1)
                    a.wait_ge(s_xn, t + 1)
                    a.dma_start(xn_d[t * P:(t + 1) * P, :], xn[:, t, :]).then_inc(s_xnd, 16)
                if n == T1 + NT - 1:
                    a.wait_ge(s_sub, 1)
                    a.activation(pr[:, :, :], lg[:, :, :], ACT.Exp).then_inc(s_exp, 1)
                if second(n - 2):
                    y_out(n - 2 - N2)
                for u in SPLIT_AT.get(n, []):
                    if (u, 0) not in HI_AT.values():
                        split_hi(u)
                if n in HI_AT:
                    u, m = HI_AT[n]
                    split_hi(u, (m,))
            a.wait_ge(s_mm2, N3)
            for q, t in enumerate(BY_PE):
                if q >= 2:
                    a.wait_ge(s_sum, q - 1)
                for k in range(TOPK):
                    ins = a.activation(diag[:, q % 2, k, :], ident, ACT.Copy, scale=wk[:, k, t:t + 1])
                ins.then_inc(s_diag, 1)

        @block.tensor
        def _(pe):
            W1 = {}

            def x_transpose(g):
                if g < T1:
                    pe.wait_ge(s_xn1, g + 1)
                    src = xg[:, g % G, :]
                elif g < GB:
                    pe.wait_ge(s_xn, g - T1 + 1)
                    src = xn[:, g - T1, :]
                else:
                    j = g - GB
                    pe.wait_ge(*rows_sem(j))
                    src = rows_of(j)
                if g >= 1:
                    pe.wait_ge(s_xlo, g)
                pe.transpose(psX[:, 0:P], src[:, 0:P], ident)
                pe.transpose(psX[:, P:D], src[:, P:D], ident).then_inc(s_xt, 1)

            def weights(n, rows, first, count):
                if n < T1:
                    return cw[0:rows, bass.ds(W1[n], 1), :, :].rearrange("p o h n -> p (o h n)")[:, first:first + count]
                if not second(n):
                    return W[0:rows, SHARED_SLOT[shared_step(n)[0]], first:first + count]
                return W[0:rows, bass.ds(W1[n], 1), first:first + count].rearrange("p o n -> p (o n)")

            def load_expert(n):
                if n < T1:
                    W1[n] = pe.value_load(tile1[0:1, 0, n:n + 1], min_val=0, max_val=E1 - 1)
                elif second(n):
                    j = n - N2
                    W1[n] = pe.value_load(etile[0:1, j:j + 1], min_val=0, max_val=E2 - 1)

            def inner(n):
                if n >= T1 and not second(n):
                    c, t = shared_step(n)
                    if t == 0:
                        wait_unit(pe, 2 + c)
                if second(n):
                    j = n - N2
                    if j == 0:
                        for u in (POOL_LO[-1], 2 + CH + LATE - 1):
                            wait_unit(pe, u)
                    if j % NT == 0 and 1 <= j // NT < TOPK:
                        wait_unit(pe, 2 + CH + LATE + j // NT - 1)
                if n < N2 or n == N3 - 1:
                    pe.wait_ge(s_xlo, x_group(n) + 1)
                hi, lo, width = (0, KD * D, D) if n < T1 else (0, KD * 2 * I2, 2 * I2)
                o, slot = psG[n % 2][:, 0:width], x_slot(x_group(n))
                for k in range(KD):
                    b = slice(k * P, (k + 1) * P)
                    whi = weights(n, P, hi + k * width, width)
                    pe.matmul(o, xT[:, slot, 0, b], whi, start=(k == 0), stop=False)
                    pe.matmul(o, xT[:, slot, 1, b], whi, start=False, stop=False)
                    mm = pe.matmul(o, xT[:, slot, 0, b], weights(n, P, lo + k * width, width), start=False, stop=(k == KD - 1))
                mm.then_inc(s_mm1, 1)

            def transpose(n):
                u, width = n % 2, D if n < T1 else I2
                pe.wait_ge(s_hid, n + 1)
                pe.transpose(psH[u][:, 0:P], hid[:, u, 0:P], ident)
                pe.transpose(psH[u][0:width - P, P:2 * P], hid[:, u, P:width], ident).then_inc(s_ht, 1)

            def outer(n):
                pe.wait_ge(s_htlo, n + 1)
                (start, stop), y, u = y_edges(n), y_group(n), n % 2
                if start and y >= 2:
                    wait_y_read(pe, y - 2)
                o = psY(y)
                if n < T1:
                    for k in range(KD):
                        whi = weights(n, P, k * D, D)
                        pe.matmul(o, hT[:, u, 2 * k, :], whi, start=(k == 0), stop=False)
                        pe.matmul(o, hT[:, u, 2 * k + 1, :], whi, start=False, stop=False)
                        mm = pe.matmul(o, hT[:, u, 2 * k, :], weights(n, P, (KD + k) * D, D), start=False, stop=(k == KD - 1))
                    mm.then_inc(s_mm2, 1)
                    return
                R = LO + IB
                whi = weights(n, P, DA, D)
                pe.matmul(o, hT[:, u, 0, :], whi, start=start, stop=False)
                pe.matmul(o, hT[:, u, 1, :], whi, start=False, stop=False)
                pe.matmul(o, hT[:, u, 0, :], weights(n, P, DA + D, D), start=False, stop=False)
                pe.matmul(o, hT[0:R, u, 4, :], weights(n, R, DB1, D), start=False, stop=False)
                pe.matmul(o, hT[0:IB, u, 4, :], weights(n, IB, DB2, D), start=False, stop=stop).then_inc(s_mm2, 1)

            tri, one = cr[:, 0, :], cr[:, 1, :]

            def ranks(e, totals, w):
                n = NT * e
                pe.matmul(psR[:, R_RANK:R_RANK + n], tri, sel[:, 0:n], start=True, stop=False, skip_group_check=True)
                for t in range(NT - 1):
                    m = NT - 1 - t
                    pe.matmul(psR[:, R_RANK + (t + 1) * e:R_RANK + n].rearrange("p (m e) -> p m e", e=e), one,
                              sel[:, t * e:(t + 1) * e].rearrange("p (o e) -> p o e", o=1).to_broadcast([P, m, e]),
                              start=False, stop=(t == NT - 2), skip_group_check=True)
                pe.matmul(psR[:, R_TOT:R_TOT + w], one, totals, start=True, stop=True).then_inc(s_rank, 1)

            def inverse(i, cols, first, last):
                pe.wait_ge(s_ab, i + 1)
                for c in range(NT // 2):
                    mm = pe.matmul(psR[:, R_INV:R_INV + cols], bm[:, i % 2, c, :], am[:, i % 2, c, 0:cols],
                                   start=(first and c == 0), stop=(last and c == NT // 2 - 1))
                mm.then_inc(s_inv, 1)

            def logits(t):
                if t == 0:
                    pe.wait_ge(s_rwlo, 1)
                pe.wait_ge(s_xlo, T1 + t + 1)
                for k in range(KD):
                    b, z = slice(k * P, (k + 1) * P), slice(k * NZ, (k + 1) * NZ)
                    o = psR[:, t * NZ:(t + 1) * NZ]
                    pe.matmul(o, xT[:, t, 0, b], rw[:, 0, z], start=(k == 0), stop=False)
                    pe.matmul(o, xT[:, t, 0, b], rw[:, 1, z], start=False, stop=False)
                    mm = pe.matmul(o, xT[:, t, 1, b], rw[:, 0, z], start=False, stop=(k == KD - 1))
                mm.then_inc(s_lgt, 1)

            pe.wait_ge(s_cr, 1)
            pe.wait_ge(s_sel, 1)
            ranks(E1, lt[:, :, :].rearrange("p t e -> p (t e)"), NT * S1)
            inverse(0, NT, True, False)
            inverse(1, NT, False, True)
            for i in range(WARM):
                pe.matmul(psG[0][:, 0:D], one, cr[:, :, :].rearrange("p a n -> p (a n)"), start=True, stop=True)
            pe.wait_ge(s_ca, 16)
            x_transpose(0)
            wait_unit(pe, 1)
            pe.wait_ge(s_pairs, 1)
            load_expert(0)
            for n in range(N + 2):
                if n < N:
                    inner(n)
                if n == N2 - 2:
                    pe.wait_ge(s_et, 1)
                if n + 1 < N:
                    load_expert(n + 1)
                if 1 <= n <= N:
                    transpose(n - 1)
                if T1 <= n < T1 + NT:
                    logits(n - T1)
                for g in x_at(n):
                    x_transpose(g)
                if n == T1 + RANKS_AT:
                    pe.wait_ge(s_sel, 2)
                    ranks(E2, sel[:, :], NT * E2)
                if n == T1 + RANKS_AT + 2:
                    pe.wait_ge(s_started, 1)
                    pe.matmul(psR[:, R_TOT:R_TOT + J2], one[0:E2, :], started[:, :], start=True, stop=True).then_inc(s_count, 1)
                if 0 <= n - T1 - INVERSE_AT < 2 * TOPK:
                    i = n - T1 - INVERSE_AT
                    inverse(2 + i, J2, i == 0, i == 2 * TOPK - 1)
                if n >= 2:
                    outer(n - 2)

            for q, t in enumerate(BY_PE):
                pe.wait_ge(s_diag, q + 1)
                pe.wait_ge(s_fin[t], 16)
                if q >= 2:
                    pe.wait_ge(s_comb, t - 3)
                else:
                    pe.wait_ge(s_hid, N)
                for k in range(TOPK):
                    mm = pe.matmul(psG[q % 2][:, 0:D], diag[:, q % 2, k, :], fin[:, t, k, :], start=(k == 0), stop=(k == TOPK - 1))
                mm.then_inc(s_sum, 1)

        @block.vector
        def _(v):
            done = [0]

            def step(ins, more=()):
                for i in (ins, *more):
                    i.then_inc(s_v, 1)
                    done[0] += 1
                v.wait_ge(s_v, done[0])

            seen = {}

            def stats_of(h, t):
                v.bn_stats(stats[:, t, :], (xs if h else xn)[:, t, :]).then_inc(s_v, 1)
                done[0] += 1
                seen[h, t] = done[0]

            def mean_of(h, t):
                v.wait_ge(s_v, seen[h, t])
                v.bn_aggr(mv[:, h, t, :], stats[:, t, :]).then_inc(s_v, 1)
                done[0] += 1
                seen[h, t] = done[0]

            def var_of(h, t):
                v.wait_ge(s_v, seen[h, t])
                v.tensor_scalar(mv[:, h, t, 1:2], mv[:, h, t, 1:2], EPS, None, ALU.add).then_inc(s_var, 1)

            def shift_of(h, t):
                v.wait_ge(s_rstd, h * NT + t + 1)
                v.scalar_tensor_tensor(shift[:, h, t:t + 1], mv[:, h, t, 0:1], -1.0, rstd[:, h, t:t + 1], ALU.mult, ALU.mult).then_inc(s_shift2 if h else s_shift, 1)

            def split_lo(u):
                v.wait_ge(s_whi, u + 1)
                for dst, hi, src in lo_parts(u):
                    ins = v.tensor_tensor(dst, src, f32(hi), ALU.subtract)
                ins.then_inc(s_wlo, 1)

            def split_lo_part(u, m):
                v.wait_ge(s_whi, u + 1)
                dst, hi, src = lo_parts(u)[m]
                ins = v.tensor_tensor(dst, src, f32(hi), ALU.subtract)
                if m == 2:
                    ins.then_inc(s_wlo, 1)

            def x_lo(g):
                v.wait_ge(s_xhi, g + 1)
                slot = x_slot(g)
                v.tensor_tensor(xT[:, slot, 1, :], psX[:, 0:D], f32(xT[:, slot, 0, :]), ALU.subtract).then_inc(s_xlo, 1)

            def hidden(n):
                u, up, width = (n % 2, 0, D) if n < T1 else (n % 2, I2, I2)
                v.wait_ge(s_act, n + 1)
                if n >= 2:
                    v.wait_ge(s_ht, n - 1)
                v.tensor_tensor(hid[:, u, 0:width], act[:, u, 0:width], psG[u][:, up:up + width], ALU.mult).then_inc(s_hid, 1)

            def hT_lo(n):
                u = n % 2
                v.wait_ge(s_hthi, n + 1)
                if n < T1:
                    both = hT[:, u, 0:4, :].rearrange("p (k h) n -> p k h n", h=2)
                    v.tensor_tensor(both[:, :, 1, :], psH[u][:, 0:D].rearrange("p (k n) -> p k n", k=KD), f32(both[:, :, 0, :]), ALU.subtract).then_inc(s_htlo, 1)
                else:
                    v.tensor_tensor(hT[:, u, 1, :], psH[u][:, 0:P], f32(hT[:, u, 0, :]), ALU.subtract)
                    v.tensor_tensor(hT[LO:LO + IB, u, 4, :], psH[u][0:IB, P:2 * P], f32(hT[0:IB, u, 4, :]), ALU.subtract).then_inc(s_htlo, 1)

            def add_first(n):
                t = v.value_load(tile1[0:1, 1, n:n + 1], min_val=0, max_val=NT - 1)
                v.wait_ge(s_mm2, n + 1)
                if n < NT:
                    v.wait_ge(s_xs[n], 16)
                if n >= 1:
                    v.wait_ge(s_yacc, n)
                to = xs[:, bass.ds(t, 1), :].rearrange("p o n -> p (o n)")
                v.scalar_tensor_tensor(to, psY(n), mask[:, n:n + 1], to, ALU.mult, ALU.add).then_inc(s_yacc, 1)

            def add_shared(n):
                c, t = shared_step(n)
                if c >= CA - 1:
                    v.wait_ge(s_mm2, n + 1)
                    v.wait_ge(s_yacc, T1 + t + 1 if c == CA else T1)
                    v.scalar_tensor_tensor(xs[:, t, :], psY(y_group(n)), wse[:, t:t + 1], xs[:, t, :], ALU.mult, ALU.add).then_inc(s_yacc, 1)

            iota = cb[:, C_IOTA:C_IOTA + P]
            by = lambda ap, e: ap.rearrange("p (t e) -> p t e", e=e)
            t3 = lambda ap: by(ap, E2)

            def one_hots(i, c0, cols, rows):
                c, n = slice(c0, c0 + NT // 2), NT // 2
                if i >= 2:
                    v.wait_ge(s_inv, i - 1)
                a = am[:, i % 2, :, 0:cols]
                step(v.tensor_tensor(a, mid(cb[:, C_START:C_START + cols], n, cols), last(start[:, c], n, cols), ALU.is_equal))
                v.tensor_tensor(a, f32(a), last(cb[:, rows + c0:rows + c0 + n], n, cols), ALU.mult)
                v.tensor_tensor(bm[:, i % 2, :, :], mid(iota, n, P), last(posj[:, c], n, P), ALU.is_equal).then_inc(s_ab, 1)

            def places(k):
                c = slice(0, k * NT)
                step(v.tensor_scalar(posj[:, c], posi[:, c], P - 1, None, ALU.bitwise_and))
                step(v.tensor_tensor(start[:, c], posi[:, c], posj[:, c], ALU.subtract))

            v.memset(f32(hT[32:LO, :, 4, :]), 0.0).then_inc(s_zero, 1)
            v.wait_ge(s_tok, 16)
            v.wait_ge(s_cb, 16)
            step(v.tensor_tensor(lt[:, :, :], last(tsb[:, :], NT, S1), mid(cb[:, C_THR:C_THR + S1], NT, S1), ALU.is_lt))
            w1 = NT * E1
            v.tensor_tensor(by(sel[:, 0:w1], E1), f32(lt[:, :, 1:E1 + 1]), f32(lt[:, :, 0:E1]), ALU.subtract).then_inc(s_sel, 1)
            v.wait_ge(s_rank, 1)
            step(v.tensor_reduce(starts[:, :], psR[:, R_TOT:R_TOT + NT * S1].rearrange("p (t e) -> p e t", e=S1), AX.X, ALU.add))
            step(v.tensor_tensor(by(key[:, 0:w1], E1), by(psR[:, R_RANK:R_RANK + w1], E1), mid(starts[:, 0:E1], NT, E1), ALU.add))
            step(v.tensor_tensor(eq[:, 0:w1], key[:, 0:w1], f32(sel[:, 0:w1]), ALU.mult))
            step(v.tensor_reduce(posi[:, 0:NT], by(eq[:, 0:w1], E1), AX.X, ALU.max))
            places(1)
            one_hots(0, 0, NT, C_ROW1)
            one_hots(1, NT // 2, NT, C_ROW1)
            S, m = starts[:, 1:E1], E1 - 1
            c8 = key[:, 0:m * NT].rearrange("p (e k) -> p e k", k=NT)
            step(v.tensor_tensor(c8, mid(cb[:, C_START:C_START + NT], m, NT), last(S, m, NT), ALU.is_le))
            step(v.tensor_reduce(mx[:, 0:m], c8, AX.X, ALU.add))
            v.wait_ge(s_inv, 2)
            v.tensor_copy(gidx[:, :], psR[:, R_INV:R_INV + NT]).then_inc(s_idx, 1)
            step(v.tensor_tensor(mx[:, 0:m], mx[:, 0:m], iota[:, 0:m], ALU.add))
            step(v.tensor_tensor(sm3[:, :, :], mid(mx[:, 0:m], J1, m), last(iota[:, 0:J1], J1, m), ALU.is_le))
            step(v.tensor_reduce(sm[:, 0, :], sm3[:, :, :], AX.X, ALU.add))
            step(v.tensor_tensor(sm[:, 1, :], iota[:, 0:J1], sm[:, 0, :], ALU.subtract))
            v.wait_ge(s_ca, 16)
            step(v.tensor_copy(tile1[:, :, :], sm[:, 0:2, :]),
                 [v.tensor_scalar(sm[:, 2, :], sm[:, 1, :], float(P), lane, ALU.mult, ALU.add)])
            step(v.tensor_tensor(sm3[:, :, :], mid(S, J1, m), last(sm[:, 2, :], J1, m), ALU.is_le))
            step(v.tensor_reduce(sm[:, 3, :], sm3[:, :, :], AX.X, ALU.add))
            step(v.tensor_tensor(mask[:, :], sm[:, 3, :], sm[:, 0, :], ALU.is_equal))
            v.wait_ge(s_tanh, 1)
            v.tensor_scalar(mask[:, :], mask[:, :], tg[:, 0:1], None, ALU.mult).then_inc(s_pairs, 1)
            v.wait_ge(s_rwhi, 1)
            v.tensor_tensor(rw[:, 1, :], rraw[:, :, :].rearrange("p k n -> p (k n)"), f32(rw[:, 0, :]), ALU.subtract).then_inc(s_rwlo, 1)

            def first_moments(t):
                v.wait_ge(s_x[t], 16)
                stats_of(0, t)
                mean_of(0, t)
                var_of(0, t)

            split_lo(1)
            first_moments(0)
            first_moments(1)
            shift_of(0, 0)
            first_moments(2)
            shift_of(0, 1)
            x_lo(0)
            first_moments(3)
            shift_of(0, 2)
            v.wait_ge(s_pairs, 1)
            v.wait_ge(s_zero, 1)

            z = psR[:, 0:NT * NZ].rearrange("p (t z) -> p t z", z=NZ)[:, :, 0:E2]
            zse = psR[:, 0:NT * NZ].rearrange("p (t z) -> p t z", z=NZ)[:, :, E2]

            def best_logits():
                v.wait_ge(s_lgt, NT)
                step(v.max(best[:, 0, :], z[:, 0, :]), [v.max(best[:, t, :], z[:, t, :]) for t in range(1, NT)])
                top = best[:, :, 0:1]
                v.tensor_scalar(lg[:, :, E2 + TOPK], zse, -1.0, None, ALU.mult)
                v.tensor_tensor(lg[:, :, 0:E2], z, top.to_broadcast([P, NT, E2]), ALU.subtract)
                v.tensor_tensor(lg[:, :, E2:E2 + TOPK], best[:, :, 0:TOPK], top.to_broadcast([P, NT, TOPK]), ALU.subtract).then_inc(s_sub, 1)
                step(v.max_index(which[:, 0, :], best[:, 0, :], z[:, 0, :]),
                     [v.max_index(which[:, t, :], best[:, t, :], z[:, t, :]) for t in range(1, NT)])

            def shared_gate():
                v.wait_ge(s_exp, 1)
                step(v.tensor_scalar(wse[:, :], pr[:, :, E2 + TOPK], 1.0, None, ALU.add))
                step(v.reciprocal(wse[:, :], wse[:, :]))
                step(v.tensor_scalar(wse[:, :], wse[:, :], tg[:, 1:2], None, ALU.mult))

            def selection():
                hot = [v.tensor_tensor(t3(oh[:, k, :]), mid(iota[:, 0:E2], NT, E2), which[:, :, k:k + 1].to_broadcast([P, NT, E2]), ALU.is_equal)
                       for k in range(TOPK)]
                step(hot[0], hot[1:])
                step(v.tensor_tensor(eq[:, :], oh[:, 0, :], oh[:, 1, :], ALU.add),
                     [v.tensor_tensor(eq2[:, :], oh[:, 2, :], oh[:, 3, :], ALU.add)])
                v.tensor_tensor(sel[:, :], eq[:, :], eq2[:, :], ALU.add).then_inc(s_sel, 1)

            def expert_weights():
                step(v.tensor_reduce(mx[:, :], pr[:, :, 0:E2], AX.X, ALU.add))
                step(v.reciprocal(mx[:, :], mx[:, :]))
                step(v.tensor_scalar(mx[:, :], mx[:, :], tg[:, 1:2], None, ALU.mult))
                step(v.tensor_tensor(wk[:, :, :].rearrange("p k t -> p t k"), pr[:, :, E2:E2 + TOPK], last(mx[:, :], NT, TOPK), ALU.mult))

            def expert_tiles():
                v.wait_ge(s_rank, 2)
                step(v.tensor_reduce(cnt[:, 0, :], psR[:, R_TOT:R_TOT + NT * E2].rearrange("p (t e) -> p e t", e=E2), AX.X, ALU.add))
                step(v.tensor_scalar(cnti[:, 0, :], cnt[:, 0, :], float(P - 1), None, ALU.add))
                step(v.tensor_scalar(cnti[:, 1, :], cnti[:, 0, :], 7, None, ALU.arith_shift_right))
                step(v.tensor_tensor(t3(cum[:, :]), t3(cb[:, C_BEFORE:C_THR]), mid(cnti[:, 1, :], E2, E2), ALU.mult))
                step(v.tensor_reduce(cnt[:, 1, :], t3(cum[:, :]), AX.X, ALU.add))
                step(v.scalar_tensor_tensor(t3(key[:, :]), mid(cnt[:, 1, :], NT, E2), float(P),
                                            t3(psR[:, R_RANK:R_RANK + NT * E2]), ALU.mult, ALU.add))

            def positions(ks):
                for k in ks:
                    e = eq2 if k % 2 else eq
                    step(v.tensor_tensor(e[:, :], oh[:, k, :], key[:, :], ALU.mult))
                    step(v.tensor_reduce(posi[:, k * NT:(k + 1) * NT], t3(e[:, :]), AX.X, ALU.max))

            def sorted_rows():
                v.wait_ge(s_inv, 2 + 2 * TOPK)
                iv = psR[:, R_INV:R_INV + J2]
                step(v.tensor_scalar(inv[:, 0, :], iv, -1.0, 0.0, ALU.add, ALU.max),
                     [v.scalar_tensor_tensor(inv[:, 1, :], iv, 0.0, ca[:, P + 1:], ALU.is_equal, ALU.mult)])
                step(v.tensor_scalar(gidx2[:, :], inv[:, 0, :], 1.0, None, ALU.mult),
                     [v.tensor_tensor(didx[:, :], inv[:, 0, :], inv[:, 1, :], ALU.add)])
                v.tensor_scalar(gidx2[:, :], gidx2[:, :], TOK - 1, None, ALU.bitwise_and).then_inc(s_idx2, 1)

            def experts_started():
                step(v.tensor_tensor(cum[0:E2, 0:E2], ident[0:E2, 0:E2], cnt[0:E2, 1, :], ALU.mult))
                step(v.tensor_reduce(mx[0:E2, 0:1], cum[0:E2, 0:E2], AX.X, ALU.add))
                v.tensor_scalar(started[:, :], iota[0:E2, 0:J2], mx[0:E2, 0:1], None, ALU.is_ge).then_inc(s_started, 1)

            def tile_experts():
                v.wait_ge(s_count, 1)
                v.tensor_scalar(etile[:, :], psR[:, R_TOT:R_TOT + J2], -1.0, None, ALU.add).then_inc(s_et, 1)

            for n in range(N + 2):
                s = n - T1
                early, late = n + 4, n - E1 - 1
                if n < N:
                    hidden(n)
                if early < NT:
                    v.wait_ge(s_x[early], 16)
                    stats_of(0, early)
                if 1 <= n <= N:
                    hT_lo(n - 1)
                if early < NT:
                    mean_of(0, early)
                for g in x_at(n):
                    x_lo(g)
                if early < NT:
                    var_of(0, early)
                if n + 3 < NT:
                    shift_of(0, n + 3)
                if 2 <= n < T1 + 2:
                    add_first(n - 2)
                elif s >= NT and n - 2 < N and not second(n - 2):
                    add_shared(n - 2)
                if 0 <= late < NT:
                    v.wait_ge(s_yacc, n - 1)
                    stats_of(1, late)
                if 0 <= late - 2 < NT:
                    shift_of(1, late - 2)
                if 0 <= late < NT:
                    mean_of(1, late)
                    var_of(1, late)
                if s == NT - 1:
                    best_logits()
                    shared_gate()
                    for m in range(T1, n - 1):
                        add_shared(m)
                if s == NT:
                    selection()
                if s == NT + 1:
                    expert_weights()
                if s == RANKS_AT:
                    expert_tiles()
                    experts_started()
                if s == RANKS_AT + 1:
                    positions([0, 1])
                if s == RANKS_AT + 2:
                    positions([2, 3])
                    places(TOPK)
                if s == RANKS_AT + 3:
                    tile_experts()
                if 0 <= s - INVERSE_AT + 2 < 2 * TOPK:
                    i = s - INVERSE_AT + 2
                    one_hots(2 + i, i * NT // 2, J2, C_ROW2)
                if s == INVERSE_AT + 2 * TOPK - 1:
                    sorted_rows()
                for u in SPLIT_AT.get(n, []):
                    if u not in POOL_LO and n >= 0:
                        split_lo(u)
                if n in LO_AT:
                    split_lo_part(*LO_AT[n])
            v.wait_ge(s_yacc, YB + NT - BEFORE)
            for t in range(NT):
                if t in BY_PE:
                    v.wait_ge(s_sum, BY_PE.index(t) + 1)
                    v.tensor_tensor(xs[:, t, :], psG[BY_PE.index(t) % 2][:, 0:D], xs[:, t, :], ALU.add).then_inc(s_comb, 1)
                    continue
                v.wait_ge(s_fin[t], 16)
                for k in range(TOPK):
                    ins = v.scalar_tensor_tensor(xs[:, t, :], fin[:, t, k, :], wk[:, k, t:t + 1], xs[:, t, :], ALU.mult, ALU.add)
                    if k < TOPK - 1:
                        step(ins)
                ins.then_inc(s_comb, 1)


def kernel(x, itok_BxS_13_99985, ctx_2048, g_xattn, g_ffn, L0_ffn_router_w, L0_ffn_gate_w, L0_ffn_up_w,
           L0_ffn_down_w, L0_ffn_shared_gate_w, L0_ffn_shared_up_w, L0_ffn_shared_down_w, L0_ffn_se_gate_w):
    import numpy as np
    import concourse.bacc as bacc
    from concourse.bass_utils import run_bass_kernel_spmd

    def blocks(w):
        n, _, c = w.shape
        return w.reshape(n, KD, P, c).transpose(0, 2, 1, 3).reshape(n, P, KD * c)

    def chunks(w):
        return w.reshape(CH, I2, D)

    gate = np.concatenate([chunks(L0_ffn_shared_gate_w), L0_ffn_gate_w])
    up = np.concatenate([chunks(L0_ffn_shared_up_w), L0_ffn_up_w])
    down = np.concatenate([L0_ffn_shared_down_w.reshape(D, CH, I2).transpose(1, 2, 0), L0_ffn_down_w.transpose(0, 2, 1)])
    units = np.zeros((CH + E2, P, RAW), np.float32)
    units[:, :, 0:KD * 2 * I2] = blocks(np.concatenate([gate, up], axis=1).transpose(0, 2, 1))
    units[:, :, KD * 2 * I2:KD * 2 * I2 + D] = down[:, 0:P]
    for row in (0, LO):
        units[:, row:row + IB, KD * 2 * I2 + D:] = down[:, P:]
    ctx_t = blocks(ctx_2048.transpose(0, 2, 1)).reshape(2, 2, P, KD * D).transpose(0, 2, 1, 3).reshape(2, P, 2 * KD * D)
    router = np.concatenate([L0_ffn_router_w, L0_ffn_se_gate_w, L0_ffn_se_gate_w[:1]]).T
    lane = np.arange(P, dtype=np.float32)
    const_a = np.zeros((P, P + 1 + J2), np.float32)
    const_a[:, 0:P] = np.eye(P)
    const_a[:, P] = lane
    const_a[:, P + 1:] = (TOPK * NT + np.arange(J2)) * P + lane[:, None]
    const_b = np.zeros((P, C_END), np.float32)
    const_b[:, C_TRI:C_TRI + P] = lane[:, None] < lane
    const_b[:, C_ONE:C_ONE + P] = 1
    const_b[:, C_IOTA:C_IOTA + P] = lane
    const_b[:, C_ROW1:C_ROW1 + NT] = np.arange(NT) * P + lane[:, None]
    const_b[:, C_ROW2:C_ROW2 + TOPK * NT] = np.arange(TOPK * NT) * P + lane[:, None] + 1
    const_b[:, C_BEFORE:C_THR] = (np.arange(E2)[:, None] > np.arange(E2)).reshape(-1)
    const_b[:, C_THR:C_THR + S1] = [-2.0 ** 40] + [e * (VOCAB // E1) for e in range(1, E1)] + [2.0 ** 40] * (S1 - E1)
    const_b[:, C_START:C_END] = np.arange(J2) * P
    arrays = {
        "x": x.reshape(TOK, D),
        "tok": itok_BxS_13_99985.reshape(NT, P).T,
        "gates": np.broadcast_to(np.concatenate([g_xattn, g_ffn]), (P, 2)),
        "ctx_w": ctx_t,
        "units": units,
        "router": router.reshape(KD, P, NZ).transpose(1, 0, 2),
        "const_a": const_a,
        "const_b": const_b,
    }
    nc = bacc.Bacc("TRN2", target_bir_lowering=False, num_devices=1, dynamic_dma_scratch_size=8192)
    feed, args = {}, []
    for name, a in arrays.items():
        a = np.ascontiguousarray(a)
        feed[name] = a
        args.append(nc.dram_tensor(name, a.shape, mybir.dt.from_np(a.dtype), kind="ExternalInput").ap())
    args.append(nc.dram_tensor("out", (TOK, D), F32, kind="ExternalOutput").ap())
    moe_kernel(nc, *args)
    r = run_bass_kernel_spmd(nc, [feed], core_ids=[0])
    return r.results[0]["out"].reshape(4, 256, D)
```
